# Optimizing a Trainium2 kernel written in Bass

```python
import numpy as np
import jax
import jax.numpy as jnp

def _softmax(x, axis=-1):
    return jax.nn.softmax(x, axis=axis)

def _gelu(x):
    return jax.nn.gelu(x, approximate=True)

def _silu(x):
    return jax.nn.silu(x)

def _sigmoid(x):
    return jax.nn.sigmoid(x)

def _layernorm(x, axis=-1, eps=1e-05):
    m = jnp.mean(x, axis=axis, keepdims=True)
    v = jnp.var(x, axis=axis, keepdims=True)
    return (x - m) / jnp.sqrt(v + eps)

def _scatter_add(tgt, idx, src, axis=0):
    return tgt.at[idx].add(src)

def _segment_sum(src, seg, n):
    return jax.ops.segment_sum(src, seg, n)
kernel_name = 'mk_adj_ffn_d1_adj_r2_2bd576'

def setup_inputs(seed: int=0):
    np.random.seed(seed)
    _w = jnp.asarray

    def _rec_inputs():
        import jax
        import jax.numpy as jnp
        _gk = jax.random.key(seed)
        x = -0.000929 + 1 * jax.random.normal(jax.random.fold_in(_gk, 1), (2048, 256), jnp.float32)
        _a = jax.random.bernoulli(jax.random.fold_in(_gk, 2), 0.00195312, (2048, 2048))
        _af = _a.astype(jnp.float32)
        _af = _af * jax.random.uniform(jax.random.fold_in(_gk, 3), (2048, 2048), jnp.float32, 0.05, 5.22011)
        adj = _af
        return (x, adj)
    x, adj = _rec_inputs()

    def _L0_gnn_setup():
        import jax, jax.numpy as jnp
        import numpy as np
        N = 1024
        HID = 256
        H = 8
        key = jax.random.key(seed)
        ks = jax.random.split(key, 8)
        x = jax.random.normal(ks[0], (N, HID), dtype=jnp.float32)
        sp = jax.random.normal(ks[1], (N, N), dtype=jnp.float32)
        zero_mask = jax.random.uniform(ks[2], (N, N)) < 0.2
        spatial_encoding = jnp.where(zero_mask, 0.0, sp)
        edge_encoding = jax.random.normal(ks[3], (N, N), dtype=jnp.float32)
        s = 1.0 / np.sqrt(HID)
        Wq = jax.random.normal(ks[4], (HID, HID * H), dtype=jnp.float32) * s
        Wk = jax.random.normal(ks[5], (HID, HID * H), dtype=jnp.float32) * s
        Wv = jax.random.normal(ks[6], (HID, HID * H), dtype=jnp.float32) * s
        Wout = jax.random.normal(ks[7], (HID * H, HID), dtype=jnp.float32) * (1.0 / np.sqrt(HID * H))
        return {'x': x, 'spatial_encoding': spatial_encoding, 'edge_encoding': edge_encoding, 'Wq': Wq, 'Wk': Wk, 'Wv': Wv, 'Wout': Wout}
    _L0_gnn_all = _L0_gnn_setup()
    _L0_gnn_in = {k: v for k, v in _L0_gnn_all.items() if k in ('Wq', 'Wk', 'Wv', 'Wout')}
    del _L0_gnn_all

    def _L0_ffn_setup():
        import jax, jax.numpy as jnp
        import numpy as np
        B, S, D = (16, 1024, 256)
        E, TOP_K = (8, 2)
        H = 4 * D
        key = jax.random.key(seed)
        ks = jax.random.split(key, 8)
        x = jax.random.normal(ks[0], (B, S, D), dtype=jnp.float32)
        gate_w = jax.random.normal(ks[1], (D, E), dtype=jnp.float32) * 0.02
        gate_b = jnp.zeros((E,), dtype=jnp.float32)
        w1 = jax.random.normal(ks[2], (E, D, H), dtype=jnp.float32) * 0.02
        b1 = jnp.zeros((E, H), dtype=jnp.float32)
        w2 = jax.random.normal(ks[3], (E, H, D), dtype=jnp.float32) * 0.02
        b2 = jnp.zeros((E, D), dtype=jnp.float32)
        return {'x': x, 'gate_w': gate_w, 'gate_b': gate_b, 'w1': w1, 'b1': b1, 'w2': w2, 'b2': b2}
    _L0_ffn_all = _L0_ffn_setup()
    _L0_ffn_in = {k: v for k, v in _L0_ffn_all.items() if k in ('gate_w', 'gate_b', 'w1', 'b1', 'w2', 'b2')}
    del _L0_ffn_all
    return {'x': x, 'adj': adj, 'L0_gnn_Wq': _L0_gnn_in['Wq'], 'L0_gnn_Wk': _L0_gnn_in['Wk'], 'L0_gnn_Wv': _L0_gnn_in['Wv'], 'L0_gnn_Wout': _L0_gnn_in['Wout'], 'L0_ffn_gate_w': _L0_ffn_in['gate_w'], 'L0_ffn_gate_b': _L0_ffn_in['gate_b'], 'L0_ffn_w1': _L0_ffn_in['w1'], 'L0_ffn_b1': _L0_ffn_in['b1'], 'L0_ffn_w2': _L0_ffn_in['w2'], 'L0_ffn_b2': _L0_ffn_in['b2']}

def reference(x, adj, L0_gnn_Wq, L0_gnn_Wk, L0_gnn_Wv, L0_gnn_Wout, L0_ffn_gate_w, L0_ffn_gate_b, L0_ffn_w1, L0_ffn_b1, L0_ffn_w2, L0_ffn_b2):
    import jax
    import jax.numpy as jnp

    def _L0_gnn_ref(x, spatial_encoding, edge_encoding, Wq, Wk, Wv, Wout):
        import jax, jax.numpy as jnp
        import numpy as np
        N = 1024
        HID = 256
        H = 8
        n, d = x.shape
        h = Wq.shape[1] // d
        scale = d ** (-0.5)
        q = (x @ Wq).reshape(h, n, d)
        k = (x @ Wk).reshape(h, n, d)
        v = (x @ Wv).reshape(h, n, d)
        a = jnp.einsum('hnd,hmd->hnm', q, k) * scale
        a = a + spatial_encoding + edge_encoding
        mask = spatial_encoding == 0.0
        a = jnp.where(mask, -1000000.0, a)
        a = jax.nn.softmax(a, axis=-1)
        a = jnp.where(mask, 0.0, a)
        out = jnp.einsum('hnm,hmd->hnd', a, v)
        out = out.transpose(1, 0, 2).reshape(n, h * d)
        return out @ Wout

    def _L0_ffn_ref(x, gate_w, gate_b, w1, b1, w2, b2):
        import jax, jax.numpy as jnp
        import numpy as np
        B, S, D = (16, 1024, 256)
        E, TOP_K = (8, 2)
        H = 4 * D
        b, s, d = x.shape
        e = gate_b.shape[0]
        pooled = x.mean(axis=1)
        logits = pooled @ gate_w + gate_b
        top_v, top_i = jax.lax.top_k(logits, TOP_K)
        weights = jax.nn.softmax(top_v, axis=-1)
        w_full = jnp.zeros((b, e), dtype=x.dtype).at[jnp.arange(b)[:, None], top_i].add(weights)
        out = jnp.zeros_like(x)
        for ex in range(e):
            h = jax.nn.gelu(x @ w1[ex] + b1[ex], approximate=False)
            y = h @ w2[ex] + b2[ex]
            out = out + y * w_full[:, ex][:, None, None]
        return out
    x = x + _L0_gnn_ref(_layernorm(x, axis=-1), adj, adj, L0_gnn_Wq, L0_gnn_Wk, L0_gnn_Wv, L0_gnn_Wout)
    x = x + _L0_ffn_ref(_layernorm(x, axis=-1)[None], L0_ffn_gate_w, L0_ffn_gate_b, L0_ffn_w1, L0_ffn_b1, L0_ffn_w2, L0_ffn_b2)[0]
    return x

_drawn_inputs = setup_inputs


def setup_inputs(seed=0):
    import zlib

    import numpy as np

    out = dict(_drawn_inputs(seed))
    spreads = {'L0_ffn_gate_b': (0.0, 0.1), 'L0_ffn_b1': (0.0, 0.404), 'L0_ffn_b2': (0.0, 0.1)}
    factors = {}
    for name, (base, spread) in spreads.items():
        noise = np.random.default_rng([zlib.crc32(name.encode()), seed]).standard_normal(out[name].shape)
        drawn = base * np.exp(spread * noise) if base else spread * noise
        out[name] = jnp.asarray(drawn.astype(out[name].dtype))
    for name, factor in factors.items():
        out[name] = (out[name] * factor).astype(out[name].dtype)
    return out
```

```python
from contextlib import ExitStack

import concourse.bass as bass
from concourse import mybir

ALU = mybir.AluOpType
ACT = mybir.ActivationFunctionType
F32 = mybir.dt.float32
F16 = mybir.dt.float16
U32 = mybir.dt.uint32

P = 128
BANK = 512
HALF = 1024

W_SCALE = 64.0
K_SCALE = 0.25
Q_SCALE = 0.125
MASKED = -1.0e30
MAX_FLOOR = -1.0e6
TINY = 1.0e-30
EPS = 1e-5

SCORE_BANKS_FREE = 2
PT_BANKS = 2
PT_SLOTS = 4
BIAS_SLOTS = 2
OUT_BANKS = 2
PROJ_AHEAD = 8


def graph_attention_moe(nc, x, adj, wq, wk, wv, wout, gate_w, gate_b, w1, b1, w2, b2, out, bias_dram):
    N, D = x.shape
    H = wq.shape[1] // D
    E, _, F = w1.shape
    TOP = 2
    DC = D // P
    NT = N // P
    C = N // (N // H)
    RB = N // H
    PAIRS = NT // 2
    FC = F // P
    TOK = 512
    NQ = N // TOK
    GROUPS = N // BANK
    assert H == 8 and C == H and RB == 256 and DC == 2 and GROUPS == 4 and NT == 16

    with ExitStack() as ctx:
        def sb(name, shape, dt):
            return ctx.enter_context(nc.sbuf_tensor(name, shape, dt))

        def sem(name):
            return ctx.enter_context(nc.semaphore(name))

        xT_hi = sb("xT_hi", [P, DC, N], F16)
        xT_lo = sb("xT_lo", [P, DC, N], F16)
        w_hi = sb("w_hi", [P, 3, DC, N], F16)
        w_lo = sb("w_lo", [P, 3, DC, N], F16)
        wo_hi = sb("wo_hi", [P, H * DC, D], F16)
        wo_lo = sb("wo_lo", [P, H * DC, D], F16)
        q_mem = sb("q_mem", [P, 2, DC, N], F16)
        k_mem = sb("k_mem", [P, 2, DC, N], F16)
        qT_hi, qT_lo = q_mem[:, 0], q_mem[:, 1]
        kT_hi, kT_lo = k_mem[:, 0], k_mem[:, 1]
        vo = sb("vo", [P, NT, 2, D], F16)
        vT_hi = sb("vT_hi", [P, 2, DC, RB], F16)
        vT_lo = sb("vT_lo", [P, 2, DC, RB], F16)
        logits = sb("logits", [P, 2, N], F32)
        bias = sb("bias", [P, 2, N], F32)
        adj_raw = sb("adj_raw", [P, 2, N], F32)
        pT_hi = sb("pT_hi", [P, PT_SLOTS, BANK], F16)
        pT_lo = sb("pT_lo", [P, PT_SLOTS, BANK], F16)
        rows = sb("rows", [P, NT, D], F32)
        out_lo = sb("out_lo", [P, 2, D], F32)
        out_sum = sb("out_sum", [P, D], F32)
        ident = sb("ident", [P, P], F32)
        ones = sb("ones", [P, P], F32)
        stats = sb("stats", [P, NT, 6], F32)
        mv = sb("mv", [P, NT, 2], F32)
        ln_var = sb("ln_var", [P, NT], F32)
        ln_std = sb("ln_std", [P, NT], F32)
        ln_r = sb("ln_r", [P, NT], F32)
        ln_t = sb("ln_t", [P, NT], F32)
        ln_rstd = sb("ln_rstd", [P, NT], F32)
        max_a = sb("max_a", [P, 2], F32)
        max_b = sb("max_b", [P, 2], F32)
        negmax = sb("negmax", [P, 2], F32)
        rowsum = sb("rowsum", [P, 2], F32)
        sum_ok = sb("sum_ok", [P, 2], F32)
        rinv = sb("rinv", [P, 2], F32)
        gw = sb("gw", [P, DC, E], F32)
        gb = sb("gb", [1, E], F32)
        pooledT = sb("pooledT", [P, DC], F32)
        gate = sb("gate", [1, E], F32)
        top_v = sb("top_v", [1, 8], F32)
        top_i = sb("top_i", [1, 8], U32)
        gdiff = sb("gdiff", [1, 8], F32)
        wts = sb("wts", [1, TOP], F32)
        wts_all = sb("wts_all", [P, TOP], F32)
        b1T = sb("b1T", [P, TOP * FC], F32)

        x_nat = q_mem[:].rearrange("p a b n -> p (a b n)").bitcast(F32).rearrange("p (t d) -> p t d", t=NT)
        x_norm = k_mem[:].rearrange("p a b n -> p (a b n)").bitcast(F32).rearrange("p (t d) -> p t d", t=NT)
        stage = [logits[:, 0], logits[:, 1], bias[:, 0], bias[:, 1]]
        w_flat = w_hi[:].rearrange("p a b n -> p (a b n)")
        wl_flat = w_lo[:].rearrange("p a b n -> p (a b n)")
        w1_hi = w_flat[:, 0:TOP * DC * F].rearrange("p (e k f) -> p e k f", e=TOP, k=DC)
        w1_lo = wl_flat[:, 0:TOP * DC * F].rearrange("p (e k f) -> p e k f", e=TOP, k=DC)
        w2_hi = w_flat[:, TOP * DC * F:2 * TOP * DC * F].rearrange("p (e j d) -> p e j d", e=TOP, j=FC)
        w2_lo = wl_flat[:, TOP * DC * F:2 * TOP * DC * F].rearrange("p (e j d) -> p e j d", e=TOP, j=FC)
        hid = adj_raw[:, 0, 0:2 * TOK].rearrange("p (b n) -> p b n", b=2)
        b2_rows = adj_raw[0:1, 1, 0:TOP * D].rearrange("p (e d) -> p e d", e=TOP)
        b2_mix = adj_raw[0:1, 1, TOP * D:(TOP + 2) * D].rearrange("p (e d) -> p e d", e=2)
        b1_rows = adj_raw[0:TOP * FC, 1, HALF:HALF + P]

        psum = ctx.enter_context(nc.psum_tensor("psum", [P, 8, BANK], F32))
        PT0 = 4
        OUT0 = 6

        def bank(b):
            return psum[:, b]

        waited = sem("waited")
        x_loaded = sem("x_loaded")
        rows_loaded = sem("rows_loaded")
        stage_loaded = [sem(f"stage_loaded{i}") for i in range(4)]
        gate_loaded = sem("gate_loaded")
        consts_made = sem("consts_made")
        ln_steps = sem("ln_steps")
        std_ready = sem("std_ready")
        x_normed = sem("x_normed")
        xT_ready = sem("xT_ready")
        xT_hi_ready = sem("xT_hi_ready")
        xT_split = sem("xT_split")
        w_hi_ready = sem("w_hi_ready")
        w_split = sem("w_split")
        proj_ready = sem("proj_ready")
        proj_hi_ready = sem("proj_hi_ready")
        proj_split = sem("proj_split")
        scores_ready = sem("scores_ready")
        logits_ready = sem("logits_ready")
        negmax_ready = sem("negmax_ready")
        probs_ready = sem("probs_ready")
        pT_ready = sem("pT_ready")
        pT_hi_ready = sem("pT_hi_ready")
        pT_split = sem("pT_split")
        pT_used = sem("pT_used")
        out_lo_ready = sem("out_lo_ready")
        norm_steps = sem("norm_steps")
        rows_added = sem("rows_added")
        adj_loaded = [sem(f"adj_loaded{i}") for i in range(2)]
        mask_made = sem("mask_made")
        bias_made = sem("bias_made")
        bias_stored = [sem(f"bias_stored{i}") for i in range(2)]
        bias_loaded = [sem(f"bias_loaded{i}") for i in range(2)]
        pooled_ready = sem("pooled_ready")
        gate_steps = sem("gate_steps")
        gate_mm = sem("gate_mm")
        gate_exp = sem("gate_exp")
        experts_picked = sem("experts_picked")
        weights_bcast = sem("weights_bcast")
        e_loaded = [sem(f"e_loaded{i}") for i in range(4)]
        b_loaded = sem("b_loaded")
        e_hi_ready = sem("e_hi_ready")
        e_split = sem("e_split")
        b1T_ready = sem("b1T_ready")
        b2_ready = sem("b2_ready")
        b2_steps = sem("b2_steps")
        stats_made = sem("stats_made")
        stats_joined = sem("stats_joined")
        b1T_copied = sem("b1T_copied")
        b2_added = sem("b2_added")
        hid_ready = sem("hid_ready")
        gelu_ready = sem("gelu_ready")
        hid_hi_ready = sem("hid_hi_ready")
        hid_split = sem("hid_split")
        hid_used = sem("hid_used")
        y_added = sem("y_added")
        stored = sem("stored")

        x_rows = x.rearrange("(t p) d -> p t d", p=P)
        x_pos = x.rearrange("(s p c) d -> s p c d", s=2, p=P)
        out_pos = out.rearrange("(s p c) d -> s p c d", s=2, p=P)
        adj_pos = adj.rearrange("(s p c) m -> c s p m", s=2, p=P)
        w_pieces = [(w, k) for w in (wv, wk, wq) for k in range(DC)] + [(wout, k) for k in range(2)]
        rows_pos = [rows[:].rearrange("p (c s) d -> p s c d", s=2)[:, s] for s in range(2)]

        def piece_source(i):
            w, k = w_pieces[i]
            if w is wout:
                return wout[k * HALF:(k + 1) * HALF, :].rearrange("(j p) d -> p j d", p=P)
            return w[k * P:(k + 1) * P, :]

        def piece_parts(i):
            if i < 3 * DC:
                return w_hi[:, i // DC, i % DC], w_lo[:, i // DC, i % DC], stage[i % 4]
            j = (i - 3 * DC) * H
            st = stage[i % 4].rearrange("p (j d) -> p j d", d=D)
            return wo_hi[:, j:j + H], wo_lo[:, j:j + H], st

        def by_position(tile):
            return tile.rearrange("p (c r) -> p c r", c=C)

        def by_column(tile):
            return tile.rearrange("p (r c) -> p c r", c=C)

        block = ctx.enter_context(nc.Block())

        @block.sync
        def _(sp):
            sp.dma_start(x_nat, x_rows).then_inc(x_loaded, 16)
            for i in range(8):
                if i >= 4:
                    sp.wait_ge(w_split, i - 3)
                dst = stage[i % 4]
                if i >= 3 * DC:
                    dst = dst.rearrange("p (j d) -> p j d", d=D)
                sp.dma_start(dst, piece_source(i)).then_inc(stage_loaded[i % 4], 16)
            for s in range(2):
                sp.dma_start(rows_pos[s], x_pos[s]).then_inc(rows_loaded, 16)
            sp.dma_start(gw[:], gate_w.rearrange("(k p) e -> p k e", p=P)).then_inc(gate_loaded, 16)
            sp.dma_start(gb[:], gate_b.rearrange("(a e) -> a e", a=1)).then_inc(gate_loaded, 16)
            for t in range(2):
                sp.dma_start(adj_raw[:, t], adj_pos[0, t]).then_inc(adj_loaded[t], 16)

            with sp.Fori(0, NT // 2 - 1) as c:
                for k in range(2):
                    sp.wait_ge(bias_made, 2 * c + k + 1)
                    sp.sem_inc(waited, 1)
                    sp.dma_start(bias_dram[2 * c + k], bias[:, k]).then_inc(bias_stored[k], 16)
                    sp.dma_start(adj_raw[:, k], adj_pos[c + 1, k]).then_inc(adj_loaded[k], 16)
            for k in range(2):
                sp.wait_ge(bias_made, NT - 1 + k)
                sp.dma_start(bias_dram[NT - 2 + k], bias[:, k]).then_inc(bias_stored[k], 16)
            for k in range(2):
                sp.wait_ge(bias_stored[k], 8 * NT)
            with sp.Fori(1, H) as h:
                with sp.Fori(0, NT // 2) as c:
                    for k in range(2):
                        sp.wait_ge(negmax_ready, NT * h + 2 * c + k + 1)
                        sp.sem_inc(waited, 1)
                        sp.dma_start(bias[:, k], bias_dram[2 * c + k]).then_inc(bias_loaded[k], 16)

            sp.wait_ge(experts_picked, 1)
            sp.wait_ge(pT_ready, 4 * H * NT)
            sp.wait_ge(logits_ready, 2 * H * NT + 2)
            picked = [sp.value_load(top_i[0:1, e:e + 1], min_val=0, max_val=E - 1) for e in range(TOP)]
            for e in range(TOP):
                sp.dma_start(stage[e].rearrange("p (k f) -> p k f", k=DC),
                             w1[bass.ds(picked[e], 1)].rearrange("a (k p) f -> p (a k) f", p=P)
                             ).then_inc(e_loaded[e], 16)
            for e in range(TOP):
                sp.dma_start(b1_rows[e * FC:(e + 1) * FC, :],
                             b1[bass.ds(picked[e], 1)].rearrange("a (j p) -> (a j) p", p=P)).then_inc(b_loaded, 16)
                sp.dma_start(b2_rows[:, e], b2[bass.ds(picked[e], 1)]).then_inc(b_loaded, 16)
            for e in range(TOP):
                sp.dma_start(stage[2 + e].rearrange("p (j d) -> p j d", j=FC),
                             w2[bass.ds(picked[e], 1)].rearrange("a (j p) d -> p (a j) d", p=P)
                             ).then_inc(e_loaded[2 + e], 16)
            with sp.Fori(0, NQ) as q:
                sp.wait_ge(y_added, 4 * q + 8)
                sp.sem_inc(waited, 1)
                for s in range(2):
                    sp.dma_start(out_pos[s, :, bass.ds(2 * q, 2), :], rows_pos[s][:, bass.ds(2 * q, 2), :]
                                 ).then_inc(stored, 16)
            sp.wait_ge(stored, 32 * NQ)

        @block.gpsimd
        def _(pool):
            nc.gpsimd.memset(ident[:], 0.0).then_inc(consts_made, 1)
            nc.gpsimd.memset(ones[:], 1.0).then_inc(consts_made, 1)
            pool.wait_ge(consts_made, 2)
            nc.gpsimd.affine_select(out=ident[:], in_=ident[:], compare_op=ALU.not_equal, fill=1.0, base=0,
                                    pattern=[[-1, P]], channel_multiplier=1).then_inc(consts_made, 1)
            with pool.Fori(0, NT // 2) as c:
                for k in range(2):
                    pool.wait_ge(mask_made, 2 * c + k + 1)
                    nc.gpsimd.tensor_tensor(by_position(bias[:, k]), by_position(bias[:, k]),
                                            by_column(adj_raw[:, k]), ALU.add).then_inc(bias_made, 1)

        PROJ = 4 * C

        @block.tensor
        def _(pe):
            def three(o, a_hi, a_lo, b_hi, b_lo, first, last):
                nc.tensor.matmul(o, a_hi, b_hi, start=first, stop=False)
                nc.tensor.matmul(o, a_hi, b_lo, start=False, stop=False)
                return nc.tensor.matmul(o, a_lo, b_hi, start=False, stop=last)

            def transpose_rows(round_):
                for g in range(8):
                    pe.wait_ge(x_normed, 16 * round_ + 2 * g + 2)
                    for tt in range(2):
                        for k in range(DC):
                            mm = nc.tensor.transpose(bank(g)[:, k * 256 + tt * P:k * 256 + tt * P + P],
                                                     (x_norm if round_ == 0 else x_nat)[:, 2 * g + tt, k * P:(k + 1) * P],
                                                     ident[:])
                    mm.then_inc(xT_ready, 1)

            def project(base, h, c, k2):
                for n in range(3):
                    b = 3 * k2 + n
                    pe.wait_ge(proj_split, base + 4 * k2 + n + 1)
                    for d in range(DC):
                        for k in range(DC):
                            cols = bass.ds(c * RB + d * P, P)
                            rws = bass.ds(h * RB, RB)
                            mm = three(bank(b)[:, d * RB:(d + 1) * RB], w_hi[:, n, k, cols], w_lo[:, n, k, cols],
                                       xT_hi[:, k, rws], xT_lo[:, k, rws], k == 0, k == DC - 1)
                    mm.then_inc(proj_ready, 1)
                pe.wait_ge(rows_added, h * NT + OUT_BANKS)
                pe.wait_ge(proj_split, base + 4 * k2 + 4)
                pe.wait_ge(proj_split, base + 4 * k2 + 1 + PROJ_AHEAD)
                for s in range(2):
                    for d in range(DC):
                        wr = bass.ds(h * DC + d, 1)
                        mm = three(bank(OUT0 + k2)[:, s * D:(s + 1) * D],
                                   vT_hi[:, k2, d, s * P:(s + 1) * P], vT_lo[:, k2, d, s * P:(s + 1) * P],
                                   wo_hi[:, wr, :], wo_lo[:, wr, :], d == 0, d == DC - 1)
                mm.then_inc(proj_ready, 1)

            def scores(g, unit2, s):
                if g % 2 == 0:
                    pe.wait_ge(logits_ready, unit2 + g // 2 + 1)
                q = bass.ds(s * P, P) if not isinstance(s, int) else slice(s * P, (s + 1) * P)
                for k in range(DC):
                    mm = three(bank(g), qT_hi[:, k, q], qT_lo[:, k, q],
                               kT_hi[:, k, g * BANK:(g + 1) * BANK], kT_lo[:, k, g * BANK:(g + 1) * BANK],
                               k == 0, k == DC - 1)
                if g % 2 == 1:
                    mm.then_inc(scores_ready, 1)

            def transpose_probs(g, par, group):
                pe.wait_ge(pT_split, group + 1)
                for b in range(4):
                    mm = nc.tensor.transpose(bank(PT0 + g % 2)[:, b * P:(b + 1) * P],
                                             logits[:, par, g * BANK + b * P:g * BANK + (b + 1) * P], ident[:])
                mm.then_inc(pT_ready, 1)

            def weigh(g, par, group):
                pe.wait_ge(pT_split, group + 1 + PT_BANKS)
                for b in range(4):
                    t = 4 * g + b
                    sl = slice(b * P, (b + 1) * P)
                    nc.tensor.matmul(bank(OUT0 + par), pT_hi[:, g, sl], vo[:, t].rearrange("p a d -> p (a d)"),
                                     start=(t == 0), stop=False)
                    mm = nc.tensor.matmul(bank(OUT0 + par)[:, D:2 * D], pT_lo[:, g, sl], vo[:, t, 0],
                                          start=False, stop=(t == NT - 1))
                mm.then_inc(pT_used, 1)

            pe.wait_ge(consts_made, 3)
            transpose_rows(0)
            pe.wait_ge(xT_split, 8)
            pe.wait_ge(w_split, 8)
            with pe.Fori(0, H) as h:
                u2, g4, ub = h * (2 * NT), h * (4 * NT), h * NT
                pe.wait_ge(logits_ready, u2 + SCORE_BANKS_FREE)
                pe.wait_ge(pT_split, g4 + PT_BANKS)
                pe.sem_inc(waited, 1)
                with pe.Fori(0, C // 2) as pair:
                    c = 2 * pair
                    for k2 in range(2):
                        project(h * PROJ + c * 4, h, c + k2, k2)
                pe.wait_ge(proj_split, h * PROJ + PROJ - 1 + PROJ_AHEAD)
                for s in range(2):
                    for g in range(GROUPS):
                        scores(g, u2 + 2 * s, s)
                pe.wait_ge(proj_split, h * PROJ + PROJ + PROJ_AHEAD)
                pe.wait_ge(probs_ready, ub + 1)
                for g in range(2):
                    transpose_probs(g, 0, g4 + g)
                with pe.Fori(1, NT // 2) as pair:
                    i = 2 * pair
                    for k2 in range(2):
                        for g in range(GROUPS):
                            scores(g, u2 + 2 * i + 2 * k2, i + k2)
                            group = g4 + 4 * i + (4 * k2 + g - 8)
                            if g < 2:
                                transpose_probs(g + 2, k2, group + 2)
                            else:
                                if g == 2:
                                    pe.wait_ge(probs_ready, ub + i + k2)
                                transpose_probs(g - 2, 1 - k2, group + 2)
                            if g == 0:
                                pe.wait_ge(rows_added, ub + i + (k2 - 1))
                            weigh(g, k2, group)
                for k2 in range(2):
                    for g in range(GROUPS):
                        group = g4 + 4 * (NT - 2 + k2) + g
                        if g < 2:
                            transpose_probs(g + 2, k2, group + 2)
                        elif k2 == 0:
                            if g == 2:
                                pe.wait_ge(probs_ready, ub + NT)
                            transpose_probs(g - 2, 1, group + 2)
                        if g == 0:
                            pe.wait_ge(rows_added, ub + NT - 2 + k2 + 1)
                        weigh(g, k2, group)

            pe.wait_ge(rows_added, H * NT + OUT_BANKS)
            pe.wait_ge(pT_split, 4 * H * NT + PT_BANKS)
            transpose_rows(1)
            pe.wait_ge(xT_split, 16)
            for k in range(DC):
                for t in range(NT):
                    mm = nc.tensor.matmul(bank(0)[:, k:k + 1], x_nat[:, t, k * P:(k + 1) * P], ones[:, 0:1],
                                          start=(t == 0), stop=(t == NT - 1))
            mm.then_inc(pooled_ready, 1)
            pe.wait_ge(gate_steps, 1)
            pe.wait_ge(gate_loaded, 32)
            for k in range(DC):
                mm = nc.tensor.matmul(bank(1)[0:1, 0:E], pooledT[:, k:k + 1], gw[:, k],
                                      start=(k == 0), stop=(k == DC - 1))
            mm.then_inc(gate_mm, 1)
            pe.wait_ge(gate_steps, 7)
            nc.tensor.matmul(bank(2)[:, 0:TOP], ones[0:1, :], wts[:], start=True, stop=True).then_inc(gate_mm, 1)
            pe.wait_ge(b_loaded, 64)
            nc.tensor.transpose(bank(4)[:, 0:TOP * FC], b1_rows, ident[0:TOP * FC, 0:TOP * FC]).then_inc(b1T_ready, 1)
            pe.wait_ge(b2_steps, 2)
            nc.tensor.matmul(bank(3)[:, 0:D], ones[0:1, :], b2_mix[:, 1], start=True, stop=True).then_inc(b2_ready, 1)

            NH = TOP * FC

            def hidden(q, n):
                e, j = divmod(n, FC)
                tok = bass.ds(q * TOK, TOK)
                for k in range(DC):
                    mm = three(bank(n % 2), w1_hi[:, e, k, j * P:(j + 1) * P], w1_lo[:, e, k, j * P:(j + 1) * P],
                               xT_hi[:, k, tok], xT_lo[:, k, tok], k == 0, k == DC - 1)
                mm.then_inc(hid_ready, 1)

            pe.wait_ge(e_split, 4)
            pe.wait_ge(b1T_copied, 1)
            with pe.Fori(0, NQ) as q:
                for n in range(NH + 1):
                    if n < NH:
                        pe.wait_ge(gelu_ready, q * NH + n + 1)
                        hidden(q, n)
                    if n >= 1:
                        m = n - 1
                        e, j = divmod(m, FC)
                        if m == 0:
                            pe.wait_ge(y_added, q * 4 + 4)
                        pe.wait_ge(hid_split, q * NH + m + 1 + 2)
                        for t in range(4):
                            mm = three(bank(4 + t)[:, 0:D], pT_hi[:, m % 4, t * P:(t + 1) * P],
                                       pT_lo[:, m % 4, t * P:(t + 1) * P],
                                       w2_hi[:, e, j], w2_lo[:, e, j], m == 0, m == NH - 1)
                        mm.then_inc(hid_used, 1)

        @block.scalar
        def _(act):
            def copy_xT(round_):
                for g in range(8):
                    act.wait_ge(xT_ready, 8 * round_ + g + 1)
                    nc.scalar.activation(xT_hi[:, :, g * 256:(g + 1) * 256],
                                         bank(g).rearrange("p (k n) -> p k n", k=DC), ACT.Copy).then_inc(xT_hi_ready, 1)

            def root(n):
                act.wait_ge(ln_steps, n)
                nc.scalar.activation(ln_std[:], ln_var[:], ACT.Sqrt).then_inc(std_ready, 1)

            def copy_proj(base, c, k2):
                for n in range(4):
                    act.wait_ge(proj_ready, base + 4 * k2 + n + 1)
                    cols = bass.ds(c * RB, RB)
                    src = bank(3 * k2 + n if n < 3 else OUT0 + k2).rearrange("p (k n) -> p k n", k=2)
                    if n == 0:
                        dst, scale = vT_hi[:, k2], 1.0 / W_SCALE
                    elif n == 1:
                        dst, scale = kT_hi[:, :, cols], K_SCALE / W_SCALE
                    elif n == 2:
                        dst, scale = qT_hi[:, :, cols], Q_SCALE / W_SCALE
                    else:
                        dst, scale = vo[:, bass.ds(2 * c, 2), 0], 1.0 / W_SCALE
                    nc.scalar.activation(dst, src, ACT.Copy, scale=scale).then_inc(proj_hi_ready, 1)

            def exp_row(par, unit):
                act.wait_ge(negmax_ready, unit + 1 + BIAS_SLOTS)
                nc.scalar.activation(logits[:, par], logits[:, par], ACT.Exp, bias=negmax[:, par:par + 1],
                                     scale=1.0, accum_out=rowsum[:, par:par + 1]).then_inc(probs_ready, 1)

            def copy_pT(g, group):
                act.wait_ge(pT_used, group + 1)
                act.wait_ge(pT_ready, group + 1)
                nc.scalar.activation(pT_hi[:, g], bank(PT0 + g % 2), ACT.Copy).then_inc(pT_hi_ready, 1)

            def copy_out(par, unit, group_end):
                act.wait_ge(pT_used, group_end + PT_SLOTS)
                act.wait_ge(rows_added, unit + 1)
                nc.scalar.activation(out_lo[:, par], bank(OUT0 + par)[:, D:2 * D], ACT.Copy).then_inc(out_lo_ready, 1)

            def split_hi(i):
                hi, _, st = piece_parts(i)
                act.wait_ge(stage_loaded[i % 4], 16 * (i // 4 + 1))
                nc.scalar.activation(hi, st, ACT.Copy, scale=W_SCALE).then_inc(w_hi_ready, 1)

            def expert_hi(n):
                act.wait_ge(e_loaded[n], 16)
                if n < TOP:
                    hi, scale = w1_hi[:, n].rearrange("p k f -> p (k f)"), W_SCALE
                else:
                    hi, scale = w2_hi[:, n - TOP].rearrange("p j d -> p (j d)"), wts_all[:, n - TOP:n - TOP + 1]
                nc.scalar.activation(hi, stage[n], ACT.Copy, scale=scale).then_inc(e_hi_ready, 1)

            act.sem_inc(logits_ready, SCORE_BANKS_FREE)
            act.sem_inc(pT_split, PT_BANKS)
            act.sem_inc(negmax_ready, BIAS_SLOTS)
            act.sem_inc(pT_used, PT_SLOTS)
            act.sem_inc(rows_added, OUT_BANKS)
            act.sem_inc(proj_split, PROJ_AHEAD)

            split_hi(0)
            split_hi(1)
            root(1)
            split_hi(2)
            split_hi(3)
            copy_xT(0)
            for i in range(4, 8):
                split_hi(i)
            nc.scalar.preload_act_table(ACT.Exp)
            with act.Fori(0, H) as h:
                g4, ub = h * (4 * NT), h * NT
                with act.Fori(0, C // 2) as pair:
                    c = 2 * pair
                    for k2 in range(2):
                        copy_proj(h * PROJ + c * 4, c + k2, k2)
                exp_row(0, ub)
                for g in range(2):
                    copy_pT(g, g4 + g)
                with act.Fori(1, NT // 2) as pair:
                    i = 2 * pair
                    for k2 in range(2):
                        at = g4 + 4 * i + (4 * k2 - 8)
                        copy_pT(2, at + 2)
                        exp_row(1 - k2, ub + i + (k2 - 1))
                        copy_pT(3, at + 3)
                        copy_pT(0, at + 4)
                        copy_pT(1, at + 5)
                        copy_out(k2, ub + i + (k2 - 2), at + 4)
                for k2 in range(2):
                    at = g4 + 4 * (NT - 2 + k2)
                    copy_pT(2, at + 2)
                    if k2 == 0:
                        exp_row(1, ub + NT - 1)
                    copy_pT(3, at + 3)
                    if k2 == 0:
                        copy_pT(0, at + 4)
                        copy_pT(1, at + 5)
                    copy_out(k2, ub + NT - 2 + k2, at + 4)

            root(7)
            copy_xT(1)
            act.wait_ge(gate_steps, 4)
            nc.scalar.activation(gdiff[:, 1:2], gdiff[:, 0:1], ACT.Exp).then_inc(gate_exp, 1)
            for n in range(2 * TOP):
                if n == TOP:
                    act.wait_ge(weights_bcast, 1)
                expert_hi(n)
            act.wait_ge(b1T_copied, 1)
            act.sem_inc(gelu_ready, 2)
            act.sem_inc(hid_split, 2)
            act.sem_inc(hid_used, 4)
            act.sem_inc(y_added, 4)
            nc.scalar.preload_act_table(ACT.Gelu)
            with act.Fori(0, NQ) as q:
                for n in range(TOP * FC):
                    act.wait_ge(hid_ready, q * TOP * FC + n + 1)
                    act.wait_ge(hid_split, q * TOP * FC + n + 1)
                    nc.scalar.activation(hid[:, n % 2], bank(n % 2), ACT.Gelu, bias=b1T[:, n:n + 1],
                                         scale=1.0 / W_SCALE).then_inc(gelu_ready, 1)

        @block.vector
        def _(dve):
            def split_lo(i):
                hi, lo, st = piece_parts(i)
                dve.wait_ge(w_hi_ready, i + 1)
                nc.vector.scalar_tensor_tensor(lo, st, W_SCALE, hi, ALU.mult, ALU.subtract).then_inc(w_split, 1)

            def row_stats(src, round_):
                for t in range(NT):
                    nc.vector.bn_stats(stats[:, t], src[:, t]).then_inc(stats_made, 1)
                for t in range(NT):
                    dve.wait_ge(stats_made, NT * round_ + t + 1)
                    nc.vector.bn_aggr(mv[:, t], stats[:, t]).then_inc(stats_joined, 1)
                dve.wait_ge(stats_joined, NT * (round_ + 1))
                nc.vector.tensor_scalar(ln_var[:], mv[:, :, 1], EPS, None, ALU.add).then_inc(ln_steps, 1)

            def inverse_std(round_):
                base = 6 * round_
                dve.wait_ge(std_ready, round_ + 1)
                nc.vector.reciprocal(ln_r[:], ln_std[:]).then_inc(ln_steps, 1)
                dve.wait_ge(ln_steps, base + 2)
                nc.vector.tensor_tensor(ln_t[:], ln_r[:], ln_r[:], ALU.mult).then_inc(ln_steps, 1)
                dve.wait_ge(ln_steps, base + 3)
                nc.vector.tensor_tensor(ln_t[:], ln_t[:], ln_var[:], ALU.mult).then_inc(ln_steps, 1)
                dve.wait_ge(ln_steps, base + 4)
                nc.vector.tensor_scalar(ln_t[:], ln_t[:], -0.5, 1.5, ALU.mult, ALU.add).then_inc(ln_steps, 1)
                dve.wait_ge(ln_steps, base + 5)
                nc.vector.tensor_tensor(ln_rstd[:], ln_t[:], ln_r[:], ALU.mult).then_inc(ln_steps, 1)
                dve.wait_ge(ln_steps, base + 6)

            def normalise(dst, src):
                for t in range(NT):
                    nc.vector.tensor_scalar(dst[:, t], src[:, t], mv[:, t, 0:1], ln_rstd[:, t:t + 1],
                                            ALU.subtract, ALU.mult).then_inc(x_normed, 1)

            def split_xT(round_):
                for g in range(8):
                    dve.wait_ge(xT_hi_ready, 8 * round_ + g + 1)
                    cols = slice(g * 256, (g + 1) * 256)
                    nc.vector.tensor_tensor(xT_lo[:, :, cols], bank(g).rearrange("p (k n) -> p k n", k=DC),
                                            xT_hi[:, :, cols], ALU.subtract).then_inc(xT_split, 1)

            def split_proj(base, c, k2):
                for n in range(4):
                    dve.wait_ge(proj_hi_ready, base + 4 * k2 + n + 1)
                    cols = bass.ds(c * RB, RB)
                    src = bank(3 * k2 + n if n < 3 else OUT0 + k2).rearrange("p (k n) -> p k n", k=2)
                    if n == 0:
                        hi, lo, scale = vT_hi[:, k2], vT_lo[:, k2], 1.0 / W_SCALE
                    elif n == 1:
                        hi, lo, scale = kT_hi[:, :, cols], kT_lo[:, :, cols], K_SCALE / W_SCALE
                    elif n == 2:
                        hi, lo, scale = qT_hi[:, :, cols], qT_lo[:, :, cols], Q_SCALE / W_SCALE
                    else:
                        t = bass.ds(2 * c, 2)
                        hi, lo, scale = vo[:, t, 0], vo[:, t, 1], 1.0 / W_SCALE
                    nc.vector.scalar_tensor_tensor(lo, src, scale, hi, ALU.mult, ALU.subtract).then_inc(proj_split, 1)

            def bias_half(half, par, unit2, loaded):
                cols = slice(half * HALF, (half + 1) * HALF)
                dve.wait_ge(scores_ready, unit2 + half + 1)
                if half == 0:
                    dve.wait_ge(*loaded)
                else:
                    dve.wait_ge(logits_ready, unit2 + 1 + SCORE_BANKS_FREE)
                dve.sem_inc(waited, 1)
                nc.vector.tensor_tensor_reduce(
                    logits[:, par, cols], psum[:, 2 * half:2 * half + 2].rearrange("p b n -> p (b n)"),
                    bias[:, par, cols], 2.0, MAX_FLOOR if half == 0 else max_a[:, par:par + 1], ALU.add, ALU.max,
                    (max_a if half == 0 else max_b)[:, par:par + 1]).then_inc(logits_ready, 1)
                if half == 1:
                    dve.wait_ge(logits_ready, unit2 + 2 + SCORE_BANKS_FREE)
                    nc.vector.tensor_scalar(negmax[:, par:par + 1], max_b[:, par:par + 1], -1.0, None,
                                            ALU.mult).then_inc(negmax_ready, 1)

            def split_pT(g, group):
                dve.wait_ge(pT_hi_ready, group + 1)
                nc.vector.tensor_tensor(pT_lo[:, g], bank(PT0 + g % 2), pT_hi[:, g], ALU.subtract).then_inc(pT_split, 1)

            def add_rows(par, unit, unit3, t):
                one = slice(par, par + 1)
                nc.vector.tensor_scalar(sum_ok[:, one], rowsum[:, one], TINY, None, ALU.max).then_inc(norm_steps, 1)
                dve.wait_ge(out_lo_ready, unit + 1)
                nc.vector.tensor_tensor(out_sum[:], bank(OUT0 + par)[:, 0:D], out_lo[:, par], ALU.add).then_inc(norm_steps, 1)
                dve.wait_ge(norm_steps, unit3 + 1)
                nc.vector.reciprocal(rinv[:, one], sum_ok[:, one]).then_inc(norm_steps, 1)
                dve.wait_ge(norm_steps, unit3 + 3)
                tile = rows[:, t] if isinstance(t, int) else rows[:, bass.ds(t, 1)].rearrange("p a d -> p (a d)")
                nc.vector.scalar_tensor_tensor(tile, out_sum[:], rinv[:, one], tile, ALU.mult, ALU.add).then_inc(rows_added, 1)

            dve.wait_ge(x_loaded, 16)
            row_stats(x_nat, 0)
            split_lo(0)
            split_lo(1)
            inverse_std(0)
            normalise(x_norm, x_nat)
            split_lo(2)
            split_lo(3)
            split_xT(0)
            for i in range(4, 8):
                split_lo(i)
            dve.wait_ge(rows_loaded, 32)

            def mask(t, par, stored):
                dve.wait_ge(adj_loaded[par], 8 * (t - par) + 16)
                if stored:
                    dve.wait_ge(bias_stored[par], 8 * (t - par))
                nc.vector.tensor_scalar(by_position(bias[:, par]), by_column(adj_raw[:, par]), 0.0, MASKED,
                                        ALU.is_equal, ALU.mult).then_inc(mask_made, 1)

            def head(h, first):
                u2, g4, ub, u3 = h * (2 * NT), h * (4 * NT), h * NT, h * (3 * NT)

                def bias_there(t, par):
                    if first:
                        return bias_made, t + 1
                    return bias_loaded[par], h * (8 * NT) + 8 * t + (16 - 8 * par - 8 * NT)

                def steps(i, masks):
                    for k2 in range(2):
                        at = g4 + 4 * i + (4 * k2 - 8)
                        bias_half(1, 1 - k2, u2 + 2 * i + (2 * k2 - 2), None)
                        if k2 < masks:
                            mask(i + (k2 + 1), 1 - k2, True)
                        split_pT(2, at + 2)
                        bias_half(0, k2, u2 + 2 * i + 2 * k2, bias_there(i + k2, k2))
                        split_pT(3, at + 3)
                        split_pT(0, at + 4)
                        split_pT(1, at + 5)
                        add_rows(k2, ub + i + (k2 - 2), u3 + 3 * i + (3 * k2 - 6), i + (k2 - 2))

                with dve.Fori(0, C // 2) as pair:
                    for k2 in range(2):
                        split_proj(h * PROJ + pair * 8, 2 * pair + k2, k2)
                bias_half(0, 0, u2, bias_there(0, 0))
                bias_half(1, 0, u2, None)
                if first:
                    mask(2, 0, True)
                bias_half(0, 1, u2 + 2, bias_there(1, 1))
                split_pT(0, g4)
                split_pT(1, g4 + 1)
                if first:
                    with dve.Fori(1, NT // 2 - 1) as pair:
                        steps(2 * pair, 2)
                    steps(NT - 2, 1)
                else:
                    with dve.Fori(1, NT // 2) as pair:
                        steps(2 * pair, 0)
                for k2 in range(2):
                    at = g4 + 4 * (NT - 2 + k2)
                    if k2 == 0:
                        bias_half(1, 1, u2 + 2 * NT - 2, None)
                    for g in range(2, GROUPS):
                        split_pT(g, at + g)
                    if k2 == 0:
                        split_pT(0, at + 4)
                        split_pT(1, at + 5)
                    add_rows(k2, ub + NT - 2 + k2, u3 + 3 * (NT - 2 + k2), NT - 2 + k2)

            dve.wait_ge(w_split, 8)
            for t in range(2):
                mask(t, t, False)
            head(0, True)
            with dve.Fori(1, H) as h:
                head(h, False)

            dve.wait_ge(rows_added, H * NT + OUT_BANKS)
            row_stats(rows, 1)
            inverse_std(1)
            normalise(x_nat, rows)
            split_xT(1)
            dve.wait_ge(pooled_ready, 1)
            nc.vector.tensor_scalar(pooledT[:], bank(0)[:, 0:DC], 1.0 / N, None, ALU.mult).then_inc(gate_steps, 1)
            dve.wait_ge(gate_mm, 1)
            nc.vector.tensor_tensor(gate[:], bank(1)[0:1, 0:E], gb[:], ALU.add).then_inc(gate_steps, 1)
            dve.wait_ge(gate_steps, 2)
            nc.vector.max(top_v[:], gate[:]).then_inc(gate_steps, 1)
            dve.wait_ge(gate_steps, 3)
            nc.vector.max_index(top_i[:], top_v[:], gate[:]).then_inc(experts_picked, 1)
            nc.vector.tensor_tensor(gdiff[:, 0:1], top_v[:, 1:2], top_v[:, 0:1], ALU.subtract).then_inc(gate_steps, 1)
            dve.wait_ge(gate_exp, 1)
            nc.vector.tensor_scalar(gdiff[:, 2:3], gdiff[:, 1:2], 1.0, None, ALU.add).then_inc(gate_steps, 1)
            dve.wait_ge(gate_steps, 5)
            nc.vector.reciprocal(wts[:, 0:1], gdiff[:, 2:3]).then_inc(gate_steps, 1)
            dve.wait_ge(gate_steps, 6)
            nc.vector.tensor_tensor(wts[:, 1:2], gdiff[:, 1:2], wts[:, 0:1], ALU.mult).then_inc(gate_steps, 1)
            dve.wait_ge(gate_mm, 2)
            nc.vector.tensor_scalar(wts_all[:], bank(2)[:, 0:TOP], W_SCALE, None, ALU.mult).then_inc(weights_bcast, 1)
            for n in range(TOP):
                dve.wait_ge(e_hi_ready, n + 1)
                nc.vector.scalar_tensor_tensor(w1_lo[:, n].rearrange("p k f -> p (k f)"), stage[n], W_SCALE,
                                               w1_hi[:, n].rearrange("p k f -> p (k f)"),
                                               ALU.mult, ALU.subtract).then_inc(e_split, 1)
            dve.wait_ge(b1T_ready, 1)
            nc.vector.tensor_copy(b1T[:], bank(4)[:, 0:TOP * FC]).then_inc(b1T_copied, 1)
            dve.wait_ge(b_loaded, 64)
            nc.vector.tensor_scalar(b2_mix[:, 0], b2_rows[:, 0], wts[:, 0:1], None, ALU.mult).then_inc(b2_steps, 1)
            dve.wait_ge(b2_steps, 1)
            nc.vector.scalar_tensor_tensor(b2_mix[:, 1], b2_rows[:, 1], wts[:, 1:2], b2_mix[:, 0],
                                           ALU.mult, ALU.add).then_inc(b2_steps, 1)
            dve.wait_ge(weights_bcast, 1)
            for n in range(TOP):
                dve.wait_ge(e_hi_ready, TOP + n + 1)
                nc.vector.scalar_tensor_tensor(w2_lo[:, n].rearrange("p j d -> p (j d)"), stage[TOP + n],
                                               wts_all[:, n:n + 1], w2_hi[:, n].rearrange("p j d -> p (j d)"),
                                               ALU.mult, ALU.subtract).then_inc(e_split, 1)
            dve.wait_ge(b2_ready, 1)
            for t in range(NT):
                nc.vector.tensor_tensor(rows[:, t], bank(3)[:, 0:D], rows[:, t], ALU.add).then_inc(b2_added, 1)
            dve.wait_ge(b2_added, NT)
            NH = TOP * FC
            with dve.Fori(0, NQ) as q:
                for n in range(NH):
                    dve.wait_ge(hid_used, q * NH + n + 1)
                    dve.wait_ge(gelu_ready, q * NH + n + 1 + 2)
                    nc.vector.tensor_copy(pT_hi[:, n % 4], hid[:, n % 2]).then_inc(hid_hi_ready, 1)
                    dve.wait_ge(hid_hi_ready, q * NH + n + 1)
                    nc.vector.tensor_tensor(pT_lo[:, n % 4], hid[:, n % 2], pT_hi[:, n % 4],
                                            ALU.subtract).then_inc(hid_split, 1)
                dve.wait_ge(hid_used, q * NH + NH + 4)
                for t in range(4):
                    tile = rows[:, bass.ds(4 * q + t, 1)].rearrange("p a d -> p (a d)")
                    nc.vector.scalar_tensor_tensor(tile, bank(4 + t)[:, 0:D], 1.0 / W_SCALE, tile,
                                                   ALU.mult, ALU.add).then_inc(y_added, 1)


_NAMES = ["x", "adj", "L0_gnn_Wq", "L0_gnn_Wk", "L0_gnn_Wv", "L0_gnn_Wout", "L0_ffn_gate_w", "L0_ffn_gate_b",
          "L0_ffn_w1", "L0_ffn_b1", "L0_ffn_w2", "L0_ffn_b2"]


def kernel(**inputs):
    import concourse.bacc as bacc
    import numpy as np
    from concourse import mybir as _mybir
    from concourse.bass_utils import run_bass_kernel_spmd

    nc = bacc.Bacc("TRN2", target_bir_lowering=False, num_devices=1, dynamic_dma_scratch_size=1024)
    arrays, args = {}, []
    for name in _NAMES:
        a = np.ascontiguousarray(inputs[name])
        arrays[f"in_{name}"] = a
        args.append(nc.dram_tensor(f"in_{name}", a.shape, _mybir.dt.from_np(a.dtype), kind="ExternalInput").ap())
    n, d = inputs["x"].shape
    out = nc.dram_tensor("out_rows", (n, d), _mybir.dt.float32, kind="ExternalOutput").ap()
    bias = nc.dram_tensor("bias_tiles", (n // 128, 128, n), _mybir.dt.float32, kind="Internal").ap()
    graph_attention_moe(nc, *args, out, bias)
    got = run_bass_kernel_spmd(nc, [arrays], core_ids=[0])
    return got.results[0]["out_rows"]
```

```python
from contextlib import ExitStack

import concourse.bass as bass
from concourse import mybir

ALU = mybir.AluOpType
ACT = mybir.ActivationFunctionType
F32 = mybir.dt.float32
F16 = mybir.dt.float16
U32 = mybir.dt.uint32

P = 128
BANK = 512
HALF = 1024

W_SCALE = 64.0
K_SCALE = 0.25
Q_SCALE = 0.125
MASKED = -1.0e30
MAX_FLOOR = -1.0e6
TINY = 1.0e-30
EPS = 1e-5

SCORE_BANKS_FREE = 2
PT_BANKS = 2
PT_SLOTS = 4
BIAS_SLOTS = 2
OUT_BANKS = 2
PROJ_AHEAD = 8
STAGES = 8


def graph_attention_moe(nc, x, adj, wq, wk, wv, wout, gate_w, gate_b, w1, b1, w2, b2, out, bias_dram):
    N, D = x.shape
    H = wq.shape[1] // D
    E, _, F = w1.shape
    TOP = 2
    DC = D // P
    NT = N // P
    C = N // (N // H)
    RB = N // H
    FC = F // P
    EQ = 4
    NE = 2 * EQ * TOP
    TOK = 512
    NQ = N // TOK
    GROUPS = N // BANK
    assert H == 8 and C == H and RB == 256 and DC == 2 and GROUPS == 4 and NT == 16

    with ExitStack() as ctx:
        def sb(name, shape, dt):
            return ctx.enter_context(nc.sbuf_tensor(name, shape, dt))

        def sem(name):
            return ctx.enter_context(nc.semaphore(name))

        xT_hi = sb("xT_hi", [P, DC, RB], F16)
        xT_lo = sb("xT_lo", [P, DC, RB], F16)
        w_parts = sb("w_parts", [P, 2, 3, DC, N], F16)
        w_hi, w_lo = w_parts[:, 0], w_parts[:, 1]
        wo_hi = sb("wo_hi", [P, H * DC, D], F16)
        wo_lo = sb("wo_lo", [P, H * DC, D], F16)
        q_mem = sb("q_mem", [P, 2, DC, N], F16)
        k_mem = sb("k_mem", [P, 2, DC, N], F16)
        qT_hi, qT_lo = q_mem[:, 0], q_mem[:, 1]
        kT_hi, kT_lo = k_mem[:, 0], k_mem[:, 1]
        vo = sb("vo", [P, NT, 2, D], F16)
        vT_hi = sb("vT_hi", [P, 2, DC, RB], F16)
        vT_lo = sb("vT_lo", [P, 2, DC, RB], F16)
        logits = sb("logits", [P, 2, N], F32)
        bias = sb("bias", [P, 2, N], F32)
        adj_raw = sb("adj_raw", [P, 2, N], F32)
        pT_hi = sb("pT_hi", [P, PT_SLOTS, BANK], F16)
        pT_lo = sb("pT_lo", [P, PT_SLOTS, BANK], F16)
        rows = sb("rows", [P, NT, D], F32)
        out_lo = sb("out_lo", [P, 2, D], F32)
        out_sum = sb("out_sum", [P, D], F32)
        ident = sb("ident", [P, P], F32)
        ones = sb("ones", [P, P], F32)
        x_raw = sb("x_raw", [P, 2, D], F32)
        x_norm = sb("x_norm", [P, 2, D], F32)
        stats = sb("stats", [P, 2, 6], F32)
        mv = sb("mv", [P, 2, 2], F32)
        ln_v = sb("ln_v", [P, 2], F32)
        ln_r = sb("ln_r", [P, 2], F32)
        ln_t = sb("ln_t", [P, 2], F32)
        ln_u = sb("ln_u", [P, 2], F32)
        ln_w = sb("ln_w", [P, 2], F32)
        ln_rstd = sb("ln_rstd", [P, 2], F32)
        minus_half = sb("minus_half", [P, 2], F32)
        x2_sum = sb("x2_sum", [P, D], F32)
        b2_all = sb("b2_all", [P, D], F32)
        max_a = sb("max_a", [P, 2], F32)
        max_b = sb("max_b", [P, 2], F32)
        negmax = sb("negmax", [P, 2], F32)
        rowsum = sb("rowsum", [P, 2], F32)
        sum_ok = sb("sum_ok", [P, 2], F32)
        rinv = sb("rinv", [P, 2], F32)
        gw = sb("gw", [P, DC, E], F32)
        gb = sb("gb", [1, E], F32)
        pooledT = sb("pooledT", [P, DC], F32)
        gate = sb("gate", [1, E], F32)
        top_v = sb("top_v", [1, 8], F32)
        top_i = sb("top_i", [1, 8], U32)
        gdiff = sb("gdiff", [1, 8], F32)
        wts = sb("wts", [1, TOP], F32)
        wts_all = sb("wts_all", [P, TOP], F32)
        b1T = sb("b1T", [P, TOP * FC], F32)

        stage_mem = [logits[:].rearrange("p a n -> p (a n)"), bias[:].rearrange("p a n -> p (a n)")]
        stage = [stage_mem[i // 4][:, (i % 4) * HALF:(i % 4 + 1) * HALF] for i in range(STAGES)]
        w_flat = w_parts[:].rearrange("p a b c n -> p (a b c n)")
        EW = TOP * DC * F
        w1_hi, w1_lo = (w_flat[:, i * EW:(i + 1) * EW].rearrange("p (e k f) -> p e k f", e=TOP, k=DC) for i in range(2))
        w2_hi, w2_lo = (w_flat[:, i * EW:(i + 1) * EW].rearrange("p (e j d) -> p e j d", e=TOP, j=FC) for i in (2, 3))
        x2_norm = w_flat[:, 4 * EW:6 * EW].bitcast(F32).rearrange("p (t d) -> p t d", t=NT)
        x2T_hi, x2T_lo = qT_hi, qT_lo
        hid = adj_raw[:, 0, 0:2 * TOK].rearrange("p (b n) -> p b n", b=2)
        b2_rows = adj_raw[0:1, 1, 0:TOP * D].rearrange("p (e d) -> p e d", e=TOP)
        b2_mix = adj_raw[0:1, 1, TOP * D:(TOP + 2) * D].rearrange("p (e d) -> p e d", e=2)
        b1_rows = adj_raw[0:TOP * FC, 1, HALF:HALF + P]

        psum = ctx.enter_context(nc.psum_tensor("psum", [P, 8, BANK], F32))
        PT0 = 4
        OUT0 = 6
        Y0 = 2
        X2_BANKS = (4, 5, 0, 1, 2, 3, 4, 5)

        def bank(b):
            return psum[:, b]

        def pT_bank(g, last_tile):
            return bank(g if last_tile else PT0 + g % 2)


        waited = sem("waited")
        x_loaded = sem("x_loaded")
        rows_loaded = sem("rows_loaded")
        stage_loaded = [sem(f"stage_loaded{i}") for i in range(STAGES)]
        gate_loaded = sem("gate_loaded")
        consts_made = sem("consts_made")
        ln_steps = sem("ln_steps")
        x_normed = sem("x_normed")
        x2_summed = sem("x2_summed")
        b2_all_ready = sem("b2_all_ready")
        xT_ready = sem("xT_ready")
        xT_hi_ready = sem("xT_hi_ready")
        xT_split = sem("xT_split")
        w_hi_ready = sem("w_hi_ready")
        w_split = sem("w_split")
        wo_split = sem("wo_split")
        proj_ready = sem("proj_ready")
        proj_hi_ready = sem("proj_hi_ready")
        proj_split = sem("proj_split")
        scores_ready = sem("scores_ready")
        logits_ready = sem("logits_ready")
        negmax_ready = sem("negmax_ready")
        probs_ready = sem("probs_ready")
        pT_ready = sem("pT_ready")
        pT_hi_ready = sem("pT_hi_ready")
        pT_split = sem("pT_split")
        pT_used = sem("pT_used")
        out_lo_ready = sem("out_lo_ready")
        norm_steps = sem("norm_steps")
        rows_added = sem("rows_added")
        adj_loaded = [sem(f"adj_loaded{i}") for i in range(2)]
        mask_made = sem("mask_made")
        bias_made = sem("bias_made")
        bias_stored = [sem(f"bias_stored{i}") for i in range(2)]
        bias_loaded = [sem(f"bias_loaded{i}") for i in range(2)]
        pooled_ready = sem("pooled_ready")
        gate_steps = sem("gate_steps")
        gate_mm = sem("gate_mm")
        gate_exp = sem("gate_exp")
        experts_picked = sem("experts_picked")
        weights_bcast = sem("weights_bcast")
        b1_loaded = sem("b1_loaded")
        b2_loaded = sem("b2_loaded")
        e_loaded = [sem(f"e_loaded{i}") for i in range(NE)]
        e_hi_ready = sem("e_hi_ready")
        e_split = sem("e_split")
        b1T_ready = sem("b1T_ready")
        b2_ready = sem("b2_ready")
        b2_steps = sem("b2_steps")
        stats_made = sem("stats_made")
        stats_joined = sem("stats_joined")
        b1T_copied = sem("b1T_copied")
        b2_added = sem("b2_added")
        hid_ready = sem("hid_ready")
        gelu_ready = sem("gelu_ready")
        hid_hi_ready = sem("hid_hi_ready")
        hid_split = sem("hid_split")
        hid_used = sem("hid_used")
        y_ready = sem("y_ready")
        y_added = sem("y_added")
        stored = sem("stored")

        x_rows = x.rearrange("(t p) d -> p t d", p=P)
        x_pos = x.rearrange("(s p c) d -> s p c d", s=2, p=P)
        out_pos = out.rearrange("(s p c) d -> s p c d", s=2, p=P)
        adj_pos = adj.rearrange("(s p c) m -> c s p m", s=2, p=P)
        rows_pos = [rows[:].rearrange("p (c s) d -> p s c d", s=2)[:, s] for s in range(2)]

        PC = 2 * RB
        pieces = [(w, b * PC, PC) for b in range(N // PC) for w in (wv, wk, wq)]
        pieces.insert(2, (wout, 0, DC))
        pieces += [(wout, j, min(4, H * DC - j)) for j in range(DC, H * DC, 4)]
        NW = len(pieces)
        NWO = sum(w is wout for w, _, _ in pieces)

        def stage_of(i):
            return i if i < STAGES else i % (STAGES // 2)

        def piece(i):
            w, at, n = pieces[i]
            if w is wout:
                src = wout[at * P:(at + n) * P, :].rearrange("(j p) d -> p j d", p=P)
                st = stage[stage_of(i)][:, 0:n * D].rearrange("p (j d) -> p j d", j=n)
                return src, st, wo_hi[:, at:at + n], wo_lo[:, at:at + n]
            m = (wv, wk, wq).index(w)
            src = w[:, at:at + n].rearrange("(k p) m -> p k m", p=P)
            st = stage[stage_of(i)].rearrange("p (k m) -> p k m", k=DC)
            return src, st, w_hi[:, m, :, at:at + n], w_lo[:, m, :, at:at + n]

        def piece_loaded(i):
            return stage_loaded[stage_of(i)], 16 * sum(stage_of(j) == stage_of(i) for j in range(i + 1))

        def piece_split(i):
            same = sum((w is wout) == (pieces[i][0] is wout) for w, _, _ in pieces[:i + 1])
            return (wo_split if pieces[i][0] is wout else w_split), same

        QF, QJ = F // EQ, FC // EQ

        def expert_piece(i, picked=None):
            e, quarter, second = i // (2 * EQ), i % (2 * EQ) // 2, i % 2
            st = stage[i // 2][:, (i % 2) * BANK:(i % 2 + 1) * BANK]
            src = None
            if second:
                st = st.rearrange("p (j d) -> p j d", j=QJ)
                if picked:
                    rows_of = slice(quarter * QF, (quarter + 1) * QF)
                    src = w2[bass.ds(picked[e], 1), rows_of].rearrange("a (j p) d -> p (a j) d", p=P)
                js = slice(quarter * QJ, (quarter + 1) * QJ)
                return src, st, w2_hi[:, e, js], w2_lo[:, e, js]
            st = st.rearrange("p (k f) -> p k f", k=DC)
            cols = slice(quarter * QF, (quarter + 1) * QF)
            if picked:
                src = w1[bass.ds(picked[e], 1), :, cols].rearrange("a (k p) f -> p (a k) f", p=P)
            return src, st, w1_hi[:, e, :, cols], w1_lo[:, e, :, cols]

        def expert_split(n, second):
            return 2 * (n // QJ) + 1 + second

        def own_wait(engine):
            engine.sem_inc(waited, 1)

        def by_position(tile):
            return tile.rearrange("p (c r) -> p c r", c=C)

        def by_column(tile):
            return tile.rearrange("p (r c) -> p c r", c=C)

        block = ctx.enter_context(nc.Block())

        @block.sync
        def _(sp):
            def load_rows(h):
                src = x_rows[:, 2 * h:2 * h + 2] if isinstance(h, int) else x_rows[:, bass.ds(2 * h, 2)]
                sp.dma_start(x_raw[:], src).then_inc(x_loaded, 16)

            load_rows(0)
            for i in range(NW):
                before = [j for j in range(i) if stage_of(j) == stage_of(i)]
                if before:
                    sp.wait_ge(*piece_split(before[-1]))
                src, st, _, _ = piece(i)
                sp.dma_start(st, src).then_inc(piece_loaded(i)[0], 16)
                if i == STAGES - 1:
                    for t in range(2):
                        sp.dma_start(adj_raw[:, t], adj_pos[0, t]).then_inc(adj_loaded[t], 16)
            for s in range(2):
                sp.dma_start(rows_pos[s], x_pos[s]).then_inc(rows_loaded, 16)
            sp.dma_start(gw[:], gate_w.rearrange("(k p) e -> p k e", p=P)).then_inc(gate_loaded, 16)
            sp.dma_start(gb[:], gate_b.rearrange("(a e) -> a e", a=1)).then_inc(gate_loaded, 16)
            sp.wait_ge(x_normed, 2)
            load_rows(1)

            with sp.Fori(0, NT // 2 - 1) as c:
                for k in range(2):
                    sp.wait_ge(bias_made, 2 * c + k + 1)
                    own_wait(sp)
                    sp.dma_start(bias_dram[2 * c + k], bias[:, k]).then_inc(bias_stored[k], 16)
                    sp.dma_start(adj_raw[:, k], adj_pos[c + 1, k]).then_inc(adj_loaded[k], 16)
            for k in range(2):
                sp.wait_ge(bias_made, NT - 1 + k)
                sp.dma_start(bias_dram[NT - 2 + k], bias[:, k]).then_inc(bias_stored[k], 16)
            for k in range(2):
                sp.wait_ge(bias_stored[k], 8 * NT)

            def load_bias(h):
                with sp.Fori(0, NT // 2) as c:
                    for k in range(2):
                        sp.wait_ge(negmax_ready, NT * h + 2 * c + k + 1)
                        own_wait(sp)
                        sp.dma_start(bias[:, k], bias_dram[2 * c + k]).then_inc(bias_loaded[k], 16)

            with sp.Fori(1, H - 1) as h:
                sp.wait_ge(x_normed, 2 * h + 2)
                own_wait(sp)
                load_rows(h + 1)
                load_bias(h)
            load_bias(H - 1)

            sp.wait_ge(experts_picked, 1)
            sp.wait_ge(pT_ready, 4 * H * NT)
            sp.wait_ge(logits_ready, 2 * H * NT + 2)
            picked = [sp.value_load(top_i[0:1, e:e + 1], min_val=0, max_val=E - 1) for e in range(TOP)]
            for i in range(NE):
                src, st, _, _ = expert_piece(i, picked)
                sp.dma_start(st, src).then_inc(e_loaded[i], 16)
                if i == 0:
                    for e in range(TOP):
                        sp.dma_start(b1_rows[e * FC:(e + 1) * FC, :],
                                     b1[bass.ds(picked[e], 1)].rearrange("a (j p) -> (a j) p", p=P)
                                     ).then_inc(b1_loaded, 16)
                if i == 1:
                    for e in range(TOP):
                        sp.dma_start(b2_rows[:, e], b2[bass.ds(picked[e], 1)]).then_inc(b2_loaded, 16)
            with sp.Fori(0, NQ - 1) as q:
                sp.wait_ge(y_added, 4 * q + 8)
                own_wait(sp)
                for s in range(2):
                    sp.dma_start(out_pos[s, :, bass.ds(2 * q, 2), :], rows_pos[s][:, bass.ds(2 * q, 2), :]
                                 ).then_inc(stored, 16)
            for t in range(NT - 4, NT):
                sp.wait_ge(y_added, t + 5)
                sp.dma_start(out_pos[t % 2, :, t // 2, :], rows[:, t]).then_inc(stored, 16)
            sp.wait_ge(stored, 32 * (NQ - 1) + 64)

        @block.gpsimd
        def _(pool):
            nc.gpsimd.memset(ident[:], 0.0).then_inc(consts_made, 1)
            nc.gpsimd.memset(ones[:], 1.0).then_inc(consts_made, 1)
            nc.gpsimd.memset(minus_half[:], -0.5).then_inc(consts_made, 1)
            nc.gpsimd.memset(x2_sum[:], 0.0).then_inc(consts_made, 1)
            pool.wait_ge(consts_made, 4)
            nc.gpsimd.affine_select(out=ident[:], in_=ident[:], compare_op=ALU.not_equal, fill=1.0, base=0,
                                    pattern=[[-1, P]], channel_multiplier=1).then_inc(consts_made, 1)

            def power(cols, base):
                pool.wait_ge(ln_steps, base + 1)
                nc.gpsimd.tensor_tensor(ln_r[:, cols], ln_v[:, cols], minus_half[:, cols], ALU.pow).then_inc(ln_steps, 1)

            power(slice(0, 2), 0)
            with pool.Fori(0, NT // 2) as c:
                for k in range(2):
                    pool.wait_ge(mask_made, 2 * c + k + 1)
                    nc.gpsimd.tensor_tensor(by_position(bias[:, k]), by_position(bias[:, k]),
                                            by_column(adj_raw[:, k]), ALU.add).then_inc(bias_made, 1)
            with pool.Fori(1, H) as h:
                power(slice(0, 2), 6 * h)

            def second_norm(pair, k, added):
                t = 2 * pair + k
                power(slice(k, k + 1), 6 * H + 6 * t)
                if added:
                    pool.wait_ge(x_normed, 2 * H + 1 + t)
                    own_wait(pool)
                    tile = x2_norm[:, t] if isinstance(t, int) else x2_norm[:, bass.ds(t, 1)].rearrange("p a d -> p (a d)")
                    nc.gpsimd.tensor_tensor(x2_sum[:], x2_sum[:], tile, ALU.add).then_inc(x2_summed, 1)

            with pool.Fori(0, NT // 2 - 1) as pair:
                for k in range(2):
                    second_norm(pair, k, True)
            for k in range(2):
                second_norm(NT // 2 - 1, k, k == 0)
            pool.wait_ge(b2_all_ready, 1)
            for t in range(NT):
                nc.gpsimd.tensor_tensor(rows[:, t], rows[:, t], b2_all[:], ALU.add).then_inc(b2_added, 1)

        PROJ = 4 * C

        def projected(c, k2, n):
            src = bank(3 * k2 + n if n < 3 else OUT0 + k2).rearrange("p (k n) -> p k n", k=2)
            cols = bass.ds(c * RB, RB)
            t = bass.ds(2 * c, 2)
            if n == 0:
                return src, vT_hi[:, k2], vT_lo[:, k2], 1.0 / W_SCALE
            if n == 1:
                return src, kT_hi[:, :, cols], kT_lo[:, :, cols], K_SCALE / W_SCALE
            if n == 2:
                return src, qT_hi[:, :, cols], qT_lo[:, :, cols], Q_SCALE / W_SCALE
            return src, vo[:, t, 0], vo[:, t, 1], 1.0 / W_SCALE

        def interleaved(split, project_out, after_pair=None):
            i = 4
            for pair in range(C // 2):
                for n in range(8):
                    project_out(pair, n)
                    if n % 2 == 1 and i < min(NW, 4 + 3 * (pair + 1) + (n // 2 if pair == 3 else 0)):
                        split(i)
                        i += 1
                if after_pair:
                    after_pair(pair)
            while i < NW:
                split(i)
                i += 1

        @block.tensor
        def _(pe):
            def three(o, a_hi, a_lo, b_hi, b_lo, first, last):
                nc.tensor.matmul(o, a_hi, b_hi, start=first, stop=False)
                nc.tensor.matmul(o, a_hi, b_lo, start=False, stop=False)
                return nc.tensor.matmul(o, a_lo, b_hi, start=False, stop=last)

            def transpose_rows(b, two_tiles, normed):
                pe.wait_ge(x_normed, normed)
                for tt in range(2):
                    for k in range(DC):
                        mm = nc.tensor.transpose(bank(b)[:, k * RB + tt * P:k * RB + tt * P + P],
                                                 two_tiles[:, tt, k * P:(k + 1) * P], ident[:])
                mm.then_inc(xT_ready, 1)

            def project(h, pair, k2):
                base = h * PROJ + pair * 8
                c = 2 * pair + k2
                for n in range(3):
                    b = 3 * k2 + n
                    pe.wait_ge(w_split, 3 * pair + n + 1)
                    pe.wait_ge(proj_split, base + 4 * k2 + n + 1)
                    for d in range(DC):
                        for k in range(DC):
                            cols = bass.ds(c * RB + d * P, P)
                            mm = three(bank(b)[:, d * RB:(d + 1) * RB], w_hi[:, n, k, cols], w_lo[:, n, k, cols],
                                       xT_hi[:, k], xT_lo[:, k], k == 0, k == DC - 1)
                    mm.then_inc(proj_ready, 1)
                pe.wait_ge(rows_added, h * NT + OUT_BANKS)
                pe.wait_ge(proj_split, base + 4 * k2 + 4)
                pe.wait_ge(proj_split, base + 4 * k2 + 1 + PROJ_AHEAD)
                pe.wait_ge(wo_split, 1)
                for s in range(2):
                    for d in range(DC):
                        wr = bass.ds(h * DC + d, 1)
                        mm = three(bank(OUT0 + k2)[:, s * D:(s + 1) * D],
                                   vT_hi[:, k2, d, s * P:(s + 1) * P], vT_lo[:, k2, d, s * P:(s + 1) * P],
                                   wo_hi[:, wr, :], wo_lo[:, wr, :], d == 0, d == DC - 1)
                mm.then_inc(proj_ready, 1)

            def scores(g, unit2, s):
                if g % 2 == 0:
                    pe.wait_ge(logits_ready, unit2 + g // 2 + 1)
                q = bass.ds(s * P, P) if not isinstance(s, int) else slice(s * P, (s + 1) * P)
                for k in range(DC):
                    mm = three(bank(g), qT_hi[:, k, q], qT_lo[:, k, q],
                               kT_hi[:, k, g * BANK:(g + 1) * BANK], kT_lo[:, k, g * BANK:(g + 1) * BANK],
                               k == 0, k == DC - 1)
                if g % 2 == 1:
                    mm.then_inc(scores_ready, 1)

            def transpose_probs(g, par, group, last_tile=False):
                if not last_tile:
                    pe.wait_ge(pT_split, group + 1)
                for b in range(4):
                    mm = nc.tensor.transpose(pT_bank(g, last_tile)[:, b * P:(b + 1) * P],
                                             logits[:, par, g * BANK + b * P:g * BANK + (b + 1) * P], ident[:])
                mm.then_inc(pT_ready, 1)

            def weigh(g, par, group):
                pe.wait_ge(pT_split, group + 1 + PT_BANKS)
                for b in range(4):
                    t = 4 * g + b
                    sl = slice(b * P, (b + 1) * P)
                    nc.tensor.matmul(bank(OUT0 + par), pT_hi[:, g, sl], vo[:, t].rearrange("p a d -> p (a d)"),
                                     start=(t == 0), stop=False)
                    mm = nc.tensor.matmul(bank(OUT0 + par)[:, D:2 * D], pT_lo[:, g, sl], vo[:, t, 0],
                                          start=False, stop=(t == NT - 1))
                mm.then_inc(pT_used, 1)

            pe.wait_ge(consts_made, 5)
            transpose_rows(PT0, x_norm, 2)

            def head(h, last):
                u2, g4, ub = h * (2 * NT), h * (4 * NT), h * NT
                pe.wait_ge(logits_ready, u2 + SCORE_BANKS_FREE)
                pe.wait_ge(pT_split, g4 + PT_BANKS)
                pe.wait_ge(xT_split, h + 1)
                own_wait(pe)
                with pe.Fori(0, C // 2) as pair:
                    for k2 in range(2):
                        project(h, pair, k2)
                pe.wait_ge(proj_split, h * PROJ + PROJ - 2 + PROJ_AHEAD)
                for s in range(2):
                    for g in range(GROUPS):
                        scores(g, u2 + 2 * s, s)
                pe.wait_ge(proj_split, h * PROJ + PROJ + PROJ_AHEAD)
                pe.wait_ge(probs_ready, ub + 1)
                for g in range(2):
                    transpose_probs(g, 0, g4 + g)
                with pe.Fori(1, NT // 2) as pair:
                    i = 2 * pair
                    for k2 in range(2):
                        for g in range(GROUPS):
                            scores(g, u2 + 2 * i + 2 * k2, i + k2)
                            group = g4 + 4 * i + (4 * k2 + g - 8)
                            if g < 2:
                                transpose_probs(g + 2, k2, group + 2)
                            else:
                                if g == 2:
                                    pe.wait_ge(probs_ready, ub + i + k2)
                                transpose_probs(g - 2, 1 - k2, group + 2)
                            if g == 0:
                                pe.wait_ge(rows_added, ub + i + (k2 - 1))
                            weigh(g, k2, group)
                for k2 in range(2):
                    for g in range(GROUPS):
                        group = g4 + 4 * (NT - 2 + k2) + g
                        if g < 2:
                            transpose_probs(g + 2, k2, group + 2, k2 == 1)
                        elif k2 == 0:
                            if g == 2:
                                pe.wait_ge(probs_ready, ub + NT)
                                pe.wait_ge(logits_ready, u2 + 2 * NT + SCORE_BANKS_FREE)
                            transpose_probs(g - 2, 1, group + 2, True)
                        if g == 0:
                            pe.wait_ge(rows_added, ub + NT - 1 + k2)
                        if k2 == 1 and g == 2:
                            if last:
                                for group_of_rows in range(4):
                                    x2_group(group_of_rows)
                            else:
                                pe.wait_ge(wo_split, NWO)
                                transpose_rows(PT0, x_norm, 2 * h + 4)
                        weigh(g, k2, group)

            def x2_group(g):
                if g >= 6:
                    pe.wait_ge(xT_split, H + g - 5)
                transpose_rows(X2_BANKS[g], x2_norm[:, 2 * g:2 * g + 2], 2 * H + 2 * g + 2)

            with pe.Fori(0, H - 1) as h:
                head(h, False)
            head(H - 1, True)

            pe.wait_ge(pT_split, 4 * H * NT + PT_BANKS)
            for g in range(4, 7):
                x2_group(g)
            pe.wait_ge(xT_split, H + 4)
            pe.wait_ge(x2_summed, NT - 1)
            for k in range(DC):
                nc.tensor.matmul(bank(k)[:, 0:1], x2_sum[:, k * P:(k + 1) * P], ones[:, 0:1], start=True, stop=False)
            pe.wait_ge(x_normed, 2 * H + NT)
            for k in range(DC):
                mm = nc.tensor.matmul(bank(k)[:, 0:1], x2_norm[:, NT - 1, k * P:(k + 1) * P], ones[:, 0:1],
                                      start=False, stop=True)
            mm.then_inc(pooled_ready, 1)
            pe.wait_ge(rows_added, H * NT + OUT_BANKS)
            pe.wait_ge(gate_loaded, 32)
            pe.wait_ge(gate_steps, 1)
            for k in range(DC):
                mm = nc.tensor.matmul(bank(7)[0:1, 0:E], pooledT[:, k:k + 1], gw[:, k],
                                      start=(k == 0), stop=(k == DC - 1))
            mm.then_inc(gate_mm, 1)
            x2_group(7)
            pe.wait_ge(gate_steps, 7)
            nc.tensor.matmul(bank(6)[:, 8:8 + TOP], ones[0:1, :], wts[:], start=True, stop=True).then_inc(gate_mm, 1)

            NH = TOP * FC

            def hidden(q, n):
                e, j = divmod(n, FC)
                tok = bass.ds(q * TOK, TOK)
                pe.wait_ge(e_split, expert_split(n, False))
                pe.wait_ge(gelu_ready, q * NH + n + 1)
                for k in range(DC):
                    mm = three(bank(n % 2), w1_hi[:, e, k, j * P:(j + 1) * P], w1_lo[:, e, k, j * P:(j + 1) * P],
                               x2T_hi[:, k, tok], x2T_lo[:, k, tok], k == 0, k == DC - 1)
                mm.then_inc(hid_ready, 1)

            def outputs(q, m):
                e, j = divmod(m, FC)
                pe.wait_ge(hid_split, q * NH + m + 1 + 2)
                pe.wait_ge(e_split, expert_split(m, True))
                for t in range(4):
                    if m == 0:
                        pe.wait_ge(y_added, q * 4 + t + 1)
                    mm = three(bank(Y0 + t)[:, 0:D], pT_hi[:, m % 4, t * P:(t + 1) * P],
                               pT_lo[:, m % 4, t * P:(t + 1) * P],
                               w2_hi[:, e, j], w2_lo[:, e, j], m == 0, m == NH - 1)
                    if m == NH - 1 and t < 3:
                        mm.then_inc(y_ready, 1)
                mm.then_inc(hid_used, 1)

            def quarter(q, first, last):
                for n in range(1, NH + 1):
                    if n < NH:
                        hidden(q, n)
                    elif not last:
                        hidden(q + 1, 0)
                    if first and n == 2:
                        pe.wait_ge(weights_bcast, 1)
                        pe.wait_ge(b2_steps, 2)
                        nc.tensor.matmul(bank(6)[:, D:2 * D], ones[0:1, :], b2_mix[:, 1],
                                         start=True, stop=True).then_inc(b2_ready, 1)
                    outputs(q, n - 1)

            pe.wait_ge(xT_split, 2 * H)
            hidden(0, 0)
            pe.wait_ge(b1_loaded, 32)
            nc.tensor.transpose(bank(7)[:, 16:16 + TOP * FC], b1_rows, ident[0:TOP * FC, 0:TOP * FC]).then_inc(b1T_ready, 1)
            quarter(0, True, False)
            with pe.Fori(1, NQ - 1) as q:
                quarter(q, False, False)
            quarter(NQ - 1, False, True)

        @block.scalar
        def _(act):
            def copy_xT(b, dst, ready):
                act.wait_ge(xT_ready, ready)
                nc.scalar.activation(dst, bank(b).rearrange("p (k n) -> p k n", k=DC), ACT.Copy).then_inc(xT_hi_ready, 1)

            def copy_proj(base, c, n):
                k2 = n // 4
                act.wait_ge(proj_ready, base + n + 1)
                src, dst, _, scale = projected(c, k2, n % 4)
                nc.scalar.activation(dst, src, ACT.Copy, scale=scale).then_inc(proj_hi_ready, 1)

            def exp_row(par, unit):
                act.wait_ge(negmax_ready, unit + 1 + BIAS_SLOTS)
                nc.scalar.activation(logits[:, par], logits[:, par], ACT.Exp, bias=negmax[:, par:par + 1],
                                     scale=1.0, accum_out=rowsum[:, par:par + 1]).then_inc(probs_ready, 1)

            def copy_pT(g, group, last_tile=False):
                act.wait_ge(pT_used, group + 1)
                act.wait_ge(pT_ready, group + 1)
                nc.scalar.activation(pT_hi[:, g], pT_bank(g, last_tile), ACT.Copy).then_inc(pT_hi_ready, 1)

            def copy_out(par, unit, group_end):
                act.wait_ge(pT_used, group_end + PT_SLOTS)
                act.wait_ge(rows_added, unit + 1)
                nc.scalar.activation(out_lo[:, par], bank(OUT0 + par)[:, D:2 * D], ACT.Copy).then_inc(out_lo_ready, 1)

            def split_hi(i):
                _, st, hi, _ = piece(i)
                act.wait_ge(*piece_loaded(i))
                nc.scalar.activation(hi, st, ACT.Copy, scale=W_SCALE).then_inc(w_hi_ready, 1)

            def expert_hi(i):
                _, st, hi, _ = expert_piece(i)
                act.wait_ge(e_loaded[i], 16)
                scale = wts_all[:, i // (2 * EQ):i // (2 * EQ) + 1] if i % 2 else W_SCALE
                nc.scalar.activation(hi, st, ACT.Copy, scale=scale).then_inc(e_hi_ready, 1)

            act.sem_inc(logits_ready, SCORE_BANKS_FREE)
            act.sem_inc(pT_split, PT_BANKS)
            act.sem_inc(negmax_ready, BIAS_SLOTS)
            act.sem_inc(pT_used, PT_SLOTS)
            act.sem_inc(rows_added, OUT_BANKS)
            act.sem_inc(proj_split, PROJ_AHEAD)

            def head(h, first, last):
                g4, ub = h * (4 * NT), h * NT
                if first:
                    interleaved(split_hi, lambda pair, n: copy_proj(8 * pair, 2 * pair + n // 4, n))
                else:
                    with act.Fori(0, C // 2) as pair:
                        for n in range(8):
                            copy_proj(h * PROJ + 8 * pair, 2 * pair + n // 4, n)
                exp_row(0, ub)
                for g in range(2):
                    copy_pT(g, g4 + g)
                exp_row(1, ub + 1)
                with act.Fori(1, NT // 2) as pair:
                    i = 2 * pair
                    for k2 in range(2):
                        at = g4 + 4 * i + (4 * k2 - 8)
                        for n in range(4):
                            copy_pT((n + 2) % 4, at + 2 + n)
                        copy_out(k2, ub + i + (k2 - 2), at + 4)
                        exp_row(k2, ub + i + k2)
                at = g4 + 4 * (NT - 2)
                for n in range(4):
                    copy_pT((n + 2) % 4, at + 2 + n, n >= 2)
                copy_out(0, ub + NT - 2, at + 4)
                copy_pT(2, at + 6, True)
                copy_pT(3, at + 7, True)
                if last:
                    for g in range(4):
                        copy_x2T(g)
                else:
                    copy_xT(PT0, xT_hi[:], h + 2)
                copy_out(1, ub + NT - 1, at + 8)

            def copy_x2T(g):
                copy_xT(X2_BANKS[g], x2T_hi[:, :, g * RB:(g + 1) * RB], H + g + 1)

            nc.scalar.preload_act_table(ACT.Exp)
            split_hi(0)
            copy_xT(PT0, xT_hi[:], 1)
            for i in range(1, 4):
                split_hi(i)
            head(0, True, False)
            nc.scalar.preload_act_table(ACT.Exp)
            with act.Fori(1, H - 1) as h:
                head(h, False, False)
            head(H - 1, False, True)

            for g in range(4, 8):
                copy_x2T(g)
            act.wait_ge(gate_steps, 4)
            nc.scalar.activation(gdiff[:, 1:2], gdiff[:, 0:1], ACT.Exp).then_inc(gate_exp, 1)
            act.sem_inc(gelu_ready, 2)
            act.sem_inc(hid_split, 2)
            act.sem_inc(hid_used, 4)
            act.sem_inc(y_added, 4)
            nc.scalar.preload_act_table(ACT.Gelu)

            def gelu(q, n):
                act.wait_ge(hid_ready, q * TOP * FC + n + 1)
                act.wait_ge(hid_split, q * TOP * FC + n + 1)
                nc.scalar.activation(hid[:, n % 2], bank(n % 2), ACT.Gelu, bias=b1T[:, n:n + 1],
                                     scale=1.0 / W_SCALE).then_inc(gelu_ready, 1)

            expert_hi(0)
            act.wait_ge(weights_bcast, 1)
            expert_hi(1)
            expert_hi(2)
            act.wait_ge(b1T_copied, 1)
            for n in range(TOP * FC):
                gelu(0, n)
                if n + 3 < NE:
                    expert_hi(n + 3)
                if n == 3:
                    act.wait_ge(b2_ready, 1)
                    nc.scalar.activation(b2_all[:], bank(6)[:, D:2 * D], ACT.Copy).then_inc(b2_all_ready, 1)
            with act.Fori(1, NQ) as q:
                for n in range(TOP * FC):
                    gelu(q, n)

        @block.vector
        def _(dve):
            def split_lo(i):
                _, st, hi, lo = piece(i)
                dve.wait_ge(w_hi_ready, i + 1)
                nc.vector.scalar_tensor_tensor(lo, st, W_SCALE, hi, ALU.mult, ALU.subtract).then_inc(piece_split(i)[0], 1)

            def expert_lo(i):
                _, st, hi, lo = expert_piece(i)
                scale = wts_all[:, i // (2 * EQ):i // (2 * EQ) + 1] if i % 2 else W_SCALE
                dve.wait_ge(e_hi_ready, i + 1)
                nc.vector.scalar_tensor_tensor(lo, st, scale, hi, ALU.mult, ALU.subtract).then_inc(e_split, 1)

            def row_stats(src, slot, made):
                nc.vector.bn_stats(stats[:, slot], src).then_inc(stats_made, 1)
                dve.wait_ge(stats_made, made)
                own_wait(dve)
                nc.vector.bn_aggr(mv[:, slot], stats[:, slot]).then_inc(stats_joined, 1)

            def add_eps(cols, joined):
                dve.wait_ge(stats_joined, joined)
                own_wait(dve)
                nc.vector.tensor_scalar(ln_v[:, cols], mv[:, cols, 1], EPS, None, ALU.add).then_inc(ln_steps, 1)

            def inverse_std(cols, base):
                dve.wait_ge(ln_steps, base + 2)
                nc.vector.tensor_tensor(ln_t[:, cols], ln_r[:, cols], ln_r[:, cols], ALU.mult).then_inc(ln_steps, 1)
                dve.wait_ge(ln_steps, base + 3)
                nc.vector.tensor_tensor(ln_u[:, cols], ln_t[:, cols], ln_v[:, cols], ALU.mult).then_inc(ln_steps, 1)
                dve.wait_ge(ln_steps, base + 4)
                nc.vector.tensor_scalar(ln_w[:, cols], ln_u[:, cols], -0.5, 1.5, ALU.mult, ALU.add).then_inc(ln_steps, 1)
                dve.wait_ge(ln_steps, base + 5)
                nc.vector.tensor_tensor(ln_rstd[:, cols], ln_w[:, cols], ln_r[:, cols], ALU.mult).then_inc(ln_steps, 1)

            def normalise(dst, src, slot, steps):
                dve.wait_ge(ln_steps, steps)
                nc.vector.tensor_scalar(dst, src, mv[:, slot, 0:1], ln_rstd[:, slot:slot + 1],
                                        ALU.subtract, ALU.mult).then_inc(x_normed, 1)

            def head_stats(h):
                dve.wait_ge(x_loaded, 16 * h + 16)
                own_wait(dve)
                for t in range(2):
                    row_stats(x_raw[:, t], t, 2 * h + t + 1)
                add_eps(slice(0, 2), 2 * h + 2)

            def head_rows(h):
                inverse_std(slice(0, 2), 6 * h)
                for t in range(2):
                    normalise(x_norm[:, t], x_raw[:, t], t, 6 * h + 6)

            def one_tile(of, t):
                return of[:, t] if isinstance(t, int) else of[:, bass.ds(t, 1)].rearrange("p a d -> p (a d)")

            def split_xT(b, hi, lo, ready):
                dve.wait_ge(xT_hi_ready, ready)
                nc.vector.tensor_tensor(lo, bank(b).rearrange("p (k n) -> p k n", k=DC), hi,
                                        ALU.subtract).then_inc(xT_split, 1)

            def split_proj(base, c, n):
                dve.wait_ge(proj_hi_ready, base + n + 1)
                src, hi, lo, scale = projected(c, n // 4, n % 4)
                nc.vector.scalar_tensor_tensor(lo, src, scale, hi, ALU.mult, ALU.subtract).then_inc(proj_split, 1)

            def bias_half(half, par, unit2, loaded):
                cols = slice(half * HALF, (half + 1) * HALF)
                dve.wait_ge(scores_ready, unit2 + half + 1)
                if half == 0:
                    dve.wait_ge(*loaded)
                else:
                    dve.wait_ge(logits_ready, unit2 + 1 + SCORE_BANKS_FREE)
                own_wait(dve)
                nc.vector.tensor_tensor_reduce(
                    logits[:, par, cols], psum[:, 2 * half:2 * half + 2].rearrange("p b n -> p (b n)"),
                    bias[:, par, cols], 2.0, MAX_FLOOR if half == 0 else max_a[:, par:par + 1], ALU.add, ALU.max,
                    (max_a if half == 0 else max_b)[:, par:par + 1]).then_inc(logits_ready, 1)
                if half == 1:
                    dve.wait_ge(logits_ready, unit2 + 2 + SCORE_BANKS_FREE)
                    nc.vector.tensor_scalar(negmax[:, par:par + 1], max_b[:, par:par + 1], -1.0, None,
                                            ALU.mult).then_inc(negmax_ready, 1)

            def split_pT(g, group, last_tile=False):
                dve.wait_ge(pT_hi_ready, group + 1)
                nc.vector.tensor_tensor(pT_lo[:, g], pT_bank(g, last_tile), pT_hi[:, g], ALU.subtract).then_inc(pT_split, 1)

            def row_scale(par, unit3):
                one = slice(par, par + 1)
                nc.vector.tensor_scalar(sum_ok[:, one], rowsum[:, one], TINY, None, ALU.max).then_inc(norm_steps, 1)
                dve.wait_ge(norm_steps, unit3 + 1)
                nc.vector.reciprocal(rinv[:, one], sum_ok[:, one]).then_inc(norm_steps, 1)

            def add_rows(par, unit, unit3, t):
                one = slice(par, par + 1)
                dve.wait_ge(out_lo_ready, unit + 1)
                nc.vector.tensor_tensor(out_sum[:], bank(OUT0 + par)[:, 0:D], out_lo[:, par], ALU.add).then_inc(norm_steps, 1)
                dve.wait_ge(norm_steps, unit3 + 3)
                tile = one_tile(rows, t)
                nc.vector.scalar_tensor_tensor(tile, out_sum[:], rinv[:, one], tile, ALU.mult, ALU.add).then_inc(rows_added, 1)

            def mask(t, par, stored):
                dve.wait_ge(adj_loaded[par], 8 * (t - par) + 16)
                if stored:
                    dve.wait_ge(bias_stored[par], 8 * (t - par))
                nc.vector.tensor_scalar(by_position(bias[:, par]), by_column(adj_raw[:, par]), 0.0, MASKED,
                                        ALU.is_equal, ALU.mult).then_inc(mask_made, 1)

            def head(h, first, last):
                u2, g4, ub, u3 = h * (2 * NT), h * (4 * NT), h * NT, h * (3 * NT)

                def bias_there(t, par):
                    if first:
                        return bias_made, t + 1
                    return bias_loaded[par], h * (8 * NT) + 8 * t + (16 - 8 * par - 8 * NT)

                def finish(t, par):
                    add_rows(par, ub + t, u3 + 3 * t, t)
                    if last:
                        dve.wait_ge(rows_added, ub + t + 1 + OUT_BANKS)
                        own_wait(dve)
                        row_stats(one_tile(rows, t), par, 2 * H + t + 1)
                        add_eps(slice(par, par + 1), 2 * H + t + 1)

                def second_norm(t, par):
                    inverse_std(slice(par, par + 1), 6 * H + 6 * t)
                    normalise(one_tile(x2_norm, t), one_tile(rows, t), par, 6 * H + 6 * t + 6)

                def steps(i, masks, normed):
                    for k2 in range(2):
                        at = g4 + 4 * i + (4 * k2 - 8)
                        if k2 < masks:
                            mask(i + (k2 + 1), 1 - k2, True)
                        split_pT(2, at + 2)
                        row_scale(k2, u3 + 3 * i + (3 * k2 - 6))
                        if k2 >= 2 - normed:
                            second_norm(i + (k2 - 3), 1 - k2)
                        bias_half(0, k2, u2 + 2 * i + 2 * k2, bias_there(i + k2, k2))
                        split_pT(3, at + 3)
                        split_pT(0, at + 4)
                        bias_half(1, k2, u2 + 2 * i + 2 * k2, None)
                        split_pT(1, at + 5)
                        finish(i + (k2 - 2), k2)

                if first:
                    def first_masks(pair):
                        if pair in (1, 2):
                            if pair == 1:
                                dve.wait_ge(w_split, STAGES - 1)
                            mask(pair - 1, pair - 1, False)

                    interleaved(split_lo, lambda pair, n: split_proj(8 * pair, 2 * pair + n // 4, n), first_masks)
                    dve.wait_ge(w_split, NW - NWO)
                    dve.wait_ge(wo_split, NWO)
                else:
                    with dve.Fori(0, C // 2) as pair:
                        for n in range(8):
                            split_proj(h * PROJ + pair * 8, 2 * pair + n // 4, n)
                bias_half(0, 0, u2, bias_there(0, 0))
                bias_half(1, 0, u2, None)
                if first:
                    mask(2, 0, True)
                bias_half(0, 1, u2 + 2, bias_there(1, 1))
                split_pT(0, g4)
                bias_half(1, 1, u2 + 2, None)
                split_pT(1, g4 + 1)
                if first:
                    dve.wait_ge(rows_loaded, 32)
                    with dve.Fori(1, NT // 2 - 1) as pair:
                        steps(2 * pair, 2, 0)
                    steps(NT - 2, 1, 0)
                elif last:
                    steps(2, 0, 1)
                    with dve.Fori(2, NT // 2) as pair:
                        steps(2 * pair, 0, 2)
                else:
                    with dve.Fori(1, NT // 2) as pair:
                        steps(2 * pair, 0, 0)
                at = g4 + 4 * (NT - 2)
                if not last:
                    head_stats(h + 1)
                split_pT(2, at + 2)
                row_scale(0, u3 + 3 * (NT - 2))
                split_pT(3, at + 3)
                split_pT(0, at + 4, True)
                if last:
                    second_norm(NT - 3, 1)
                split_pT(1, at + 5, True)
                if not last:
                    head_rows(h + 1)
                finish(NT - 2, 0)
                split_pT(2, at + 6, True)
                row_scale(1, u3 + 3 * (NT - 1))
                split_pT(3, at + 7, True)
                if last:
                    second_norm(NT - 2, 0)
                    for g in range(4):
                        split_x2T(g)
                else:
                    split_xT(PT0, xT_hi[:], xT_lo[:], h + 2)
                finish(NT - 1, 1)
                if last:
                    second_norm(NT - 1, 1)

            def split_x2T(g):
                cols = slice(g * RB, (g + 1) * RB)
                split_xT(X2_BANKS[g], x2T_hi[:, :, cols], x2T_lo[:, :, cols], H + g + 1)

            head_stats(0)
            head_rows(0)
            split_lo(0)
            split_xT(PT0, xT_hi[:], xT_lo[:], 1)
            for i in range(1, 4):
                split_lo(i)
            head(0, True, False)
            with dve.Fori(1, H - 1) as h:
                head(h, False, False)
            head(H - 1, False, True)

            split_x2T(4)
            dve.wait_ge(pooled_ready, 1)
            nc.vector.tensor_scalar(pooledT[:], psum[:, 0:DC, 0], 1.0 / N, None, ALU.mult).then_inc(gate_steps, 1)
            dve.wait_ge(gate_mm, 1)
            nc.vector.tensor_tensor(gate[:], bank(7)[0:1, 0:E], gb[:], ALU.add).then_inc(gate_steps, 1)
            dve.wait_ge(gate_steps, 2)
            nc.vector.max(top_v[:], gate[:]).then_inc(gate_steps, 1)
            dve.wait_ge(gate_steps, 3)
            nc.vector.max_index(top_i[:], top_v[:], gate[:]).then_inc(experts_picked, 1)
            nc.vector.tensor_tensor(gdiff[:, 0:1], top_v[:, 1:2], top_v[:, 0:1], ALU.subtract).then_inc(gate_steps, 1)
            split_x2T(5)
            dve.wait_ge(gate_exp, 1)
            nc.vector.tensor_scalar(gdiff[:, 2:3], gdiff[:, 1:2], 1.0, None, ALU.add).then_inc(gate_steps, 1)
            dve.wait_ge(gate_steps, 5)
            nc.vector.reciprocal(wts[:, 0:1], gdiff[:, 2:3]).then_inc(gate_steps, 1)
            dve.wait_ge(gate_steps, 6)
            nc.vector.tensor_tensor(wts[:, 1:2], gdiff[:, 1:2], wts[:, 0:1], ALU.mult).then_inc(gate_steps, 1)
            split_x2T(6)
            split_x2T(7)
            dve.wait_ge(gate_mm, 2)
            nc.vector.tensor_scalar(wts_all[:], bank(6)[:, 8:8 + TOP], W_SCALE, None, ALU.mult).then_inc(weights_bcast, 1)
            expert_lo(0)
            dve.wait_ge(b1T_ready, 1)
            nc.vector.tensor_copy(b1T[:], bank(7)[:, 16:16 + TOP * FC]).then_inc(b1T_copied, 1)
            dve.wait_ge(weights_bcast, 1)
            expert_lo(1)
            expert_lo(2)
            NH = TOP * FC

            def split_hidden(q, n):
                dve.wait_ge(hid_used, q * NH + n + 1)
                dve.wait_ge(gelu_ready, q * NH + n + 1 + 2)
                nc.vector.tensor_copy(pT_hi[:, n % 4], hid[:, n % 2]).then_inc(hid_hi_ready, 1)
                dve.wait_ge(hid_hi_ready, q * NH + n + 1)
                nc.vector.tensor_tensor(pT_lo[:, n % 4], hid[:, n % 2], pT_hi[:, n % 4],
                                        ALU.subtract).then_inc(hid_split, 1)

            def add_experts(q):
                for t in range(4):
                    if t < 3:
                        dve.wait_ge(y_ready, 3 * q + t + 1)
                    else:
                        dve.wait_ge(hid_used, q * NH + NH + 4)
                    dve.wait_ge(b2_added, 4 * q + t + 1)
                    tile = one_tile(rows, 4 * q + t)
                    nc.vector.scalar_tensor_tensor(tile, bank(Y0 + t)[:, 0:D], 1.0 / W_SCALE, tile,
                                                   ALU.mult, ALU.add).then_inc(y_added, 1)

            for n in range(NH):
                split_hidden(0, n)
                if n == 0:
                    dve.wait_ge(b2_loaded, 32)
                    nc.vector.tensor_scalar(b2_mix[:, 0], b2_rows[:, 0], wts[:, 0:1], None, ALU.mult).then_inc(b2_steps, 1)
                    dve.wait_ge(b2_steps, 1)
                    nc.vector.scalar_tensor_tensor(b2_mix[:, 1], b2_rows[:, 1], wts[:, 1:2], b2_mix[:, 0],
                                                   ALU.mult, ALU.add).then_inc(b2_steps, 1)
                if n + 3 < NE:
                    expert_lo(n + 3)
            split_hidden(1, 0)
            add_experts(0)
            with dve.Fori(1, NQ - 1) as q:
                for n in range(1, NH):
                    split_hidden(q, n)
                split_hidden(q + 1, 0)
                add_experts(q)
            for n in range(1, NH):
                split_hidden(NQ - 1, n)
            add_experts(NQ - 1)


_NAMES = ["x", "adj", "L0_gnn_Wq", "L0_gnn_Wk", "L0_gnn_Wv", "L0_gnn_Wout", "L0_ffn_gate_w", "L0_ffn_gate_b",
          "L0_ffn_w1", "L0_ffn_b1", "L0_ffn_w2", "L0_ffn_b2"]


def kernel(**inputs):
    import concourse.bacc as bacc
    import numpy as np
    from concourse import mybir as _mybir
    from concourse.bass_utils import run_bass_kernel_spmd

    nc = bacc.Bacc("TRN2", target_bir_lowering=False, num_devices=1, dynamic_dma_scratch_size=1024)
    arrays, args = {}, []
    for name in _NAMES:
        a = np.ascontiguousarray(inputs[name])
        arrays[f"in_{name}"] = a
        args.append(nc.dram_tensor(f"in_{name}", a.shape, _mybir.dt.from_np(a.dtype), kind="ExternalInput").ap())
    n, d = inputs["x"].shape
    out = nc.dram_tensor("out_rows", (n, d), _mybir.dt.float32, kind="ExternalOutput").ap()
    bias = nc.dram_tensor("bias_tiles", (n // 128, 128, n), _mybir.dt.float32, kind="Internal").ap()
    graph_attention_moe(nc, *args, out, bias)
    got = run_bass_kernel_spmd(nc, [arrays], core_ids=[0])
    return got.results[0]["out_rows"]
```
